# Optimizing a Trainium2 kernel written in Bass

```python
import numpy as np
import jax
import jax.numpy as jnp

def _softmax(x, axis=-1):
    return jax.nn.softmax(x, axis=axis)

def _gelu(x):
    return jax.nn.gelu(x, approximate=True)

def _silu(x):
    return jax.nn.silu(x)

def _sigmoid(x):
    return jax.nn.sigmoid(x)

def _layernorm(x, axis=-1, eps=1e-05):
    m = jnp.mean(x, axis=axis, keepdims=True)
    v = jnp.var(x, axis=axis, keepdims=True)
    return (x - m) / jnp.sqrt(v + eps)

def _scatter_add(tgt, idx, src, axis=0):
    return tgt.at[idx].add(src)

def _segment_sum(src, seg, n):
    return jax.ops.segment_sum(src, seg, n)
kernel_name = 'mk_gnn_resnorm_d4_gnn_r8_b7a13d'

def setup_inputs(seed: int=0):
    np.random.seed(seed)
    _w = jnp.asarray

    def _rec_inputs():
        import jax
        import jax.numpy as jnp
        _gk = jax.random.key(seed)
        x = -0.0003713 + 1 * jax.random.normal(jax.random.fold_in(_gk, 1), (6250, 256), jnp.float32)
        src = jax.random.randint(jax.random.fold_in(_gk, 2), (100000,), 0, 6250, jnp.int32)
        dst = jnp.minimum((6250 * jax.random.uniform(jax.random.fold_in(_gk, 3), (100000,)) ** 2.0).astype(jnp.int32), 49999)
        _o = jnp.argsort(dst, stable=True)
        src = src[_o]
        dst = dst[_o]
        return (x, src, dst)
    x, src, dst = _rec_inputs()

    def _L0_gnn_setup():
        import jax, jax.numpy as jnp
        import numpy as np
        N_NODES = 6250
        N_EDGES = 100000
        DIMS = [256, 128, 64, 32, 64, 128, 256]

        def _gcn_norm(edge_index, n_nodes):
            loop = jnp.arange(n_nodes, dtype=edge_index.dtype)
            src = jnp.concatenate([edge_index[0], loop])
            dst = jnp.concatenate([edge_index[1], loop])
            deg = jax.ops.segment_sum(jnp.ones_like(dst, dtype=jnp.float32), dst, num_segments=n_nodes)
            dis = jnp.where(deg > 0, jax.lax.rsqrt(jnp.maximum(deg, 1.0)), 0.0)
            norm = dis[src] * dis[dst]
            return (src, dst, norm)

        def _gcn_layer(h, W, b, src, dst, norm, n_nodes):
            h = h @ W
            msg = h[src] * norm[:, None]
            out = jax.ops.segment_sum(msg, dst, num_segments=n_nodes)
            return out + b
        key = jax.random.key(seed)
        ks = jax.random.split(key, 2 + 2 * 6)
        x = jax.random.normal(ks[0], (N_NODES, DIMS[0]), dtype=jnp.float32)
        edge_index = jax.random.randint(ks[1], (2, N_EDGES), 0, N_NODES, dtype=jnp.int64)
        inp = {'x': x, 'edge_index': edge_index}
        for i in range(6):
            fan_in = DIMS[i]
            inp[f'W{i + 1}'] = jax.random.normal(ks[2 + i], (DIMS[i], DIMS[i + 1]), dtype=jnp.float32) * (1.0 / np.sqrt(fan_in))
            inp[f'b{i + 1}'] = jnp.zeros((DIMS[i + 1],), dtype=jnp.float32)
        return inp
    _L0_gnn_all = _L0_gnn_setup()
    _L0_gnn_in = {k: v for k, v in _L0_gnn_all.items() if k in ('W1', 'b1', 'W2', 'b2', 'W3', 'b3', 'W4', 'b4', 'W5', 'b5', 'W6', 'b6')}
    del _L0_gnn_all

    def _L1_gnn_setup():
        import jax, jax.numpy as jnp
        import numpy as np
        N_NODES = 6250
        N_EDGES = 100000
        D_IN = 256
        D_OUT = 256
        key = jax.random.key(seed)
        k1, k2, k3, k4 = jax.random.split(key, 4)
        x = jax.random.normal(k1, (N_NODES, D_IN), dtype=jnp.float32)
        edge_index = jax.random.randint(k2, (2, N_EDGES), 0, N_NODES, dtype=jnp.int64)
        glorot = (6.0 / (D_IN + D_OUT)) ** 0.5
        W = jax.random.uniform(k3, (D_OUT, D_IN), minval=-glorot, maxval=glorot, dtype=jnp.float32)
        b = jnp.zeros((D_OUT,), dtype=jnp.float32)
        return {'x': x, 'edge_index': edge_index, 'W': W, 'b': b}
    _L1_gnn_all = _L1_gnn_setup()
    _L1_gnn_in = {k: v for k, v in _L1_gnn_all.items() if k in ('W', 'b')}
    del _L1_gnn_all

    def _L2_gnn_setup():
        import jax, jax.numpy as jnp
        import numpy as np
        N, E = (6250, 100000)
        IN_DIM = 256
        OUT_DIM = 256
        H = 8
        D = OUT_DIM // H
        SCALE = D ** (-0.5)
        LN_EPS = 1e-05

        def _layernorm(x, g, b):
            mu = jnp.mean(x, axis=-1, keepdims=True)
            var = jnp.mean((x - mu) ** 2, axis=-1, keepdims=True)
            return (x - mu) * jax.lax.rsqrt(var + LN_EPS) * g + b
        key = jax.random.key(seed)
        ks = jax.random.split(key, 12)
        s = 1.0 / np.sqrt(IN_DIM)
        inp = {'x': jax.random.normal(ks[0], (N, IN_DIM), jnp.float32), 'edge_index': jax.random.randint(ks[1], (2, E), 0, N, jnp.int64), 'batch': jnp.zeros((N,), jnp.int64), 'Wq': jax.random.uniform(ks[2], (IN_DIM, OUT_DIM), jnp.float32, -s, s), 'Wk': jax.random.uniform(ks[3], (IN_DIM, OUT_DIM), jnp.float32, -s, s), 'Wv': jax.random.uniform(ks[4], (IN_DIM, OUT_DIM), jnp.float32, -s, s), 'Wo_w': jax.random.uniform(ks[5], (OUT_DIM, OUT_DIM), jnp.float32, -s, s), 'Wo_b': jnp.zeros((OUT_DIM,), jnp.float32), 'ln1_g': jnp.ones((OUT_DIM,), jnp.float32), 'ln1_b': jnp.zeros((OUT_DIM,), jnp.float32), 'ln2_g': jnp.ones((OUT_DIM,), jnp.float32), 'ln2_b': jnp.zeros((OUT_DIM,), jnp.float32), 'ffn_w1': jax.random.uniform(ks[6], (OUT_DIM, 2 * OUT_DIM), jnp.float32, -s, s), 'ffn_b1': jnp.zeros((2 * OUT_DIM,), jnp.float32), 'ffn_w2': jax.random.uniform(ks[7], (2 * OUT_DIM, OUT_DIM), jnp.float32, -s, s), 'ffn_b2': jnp.zeros((OUT_DIM,), jnp.float32)}
        return inp
    _L2_gnn_all = _L2_gnn_setup()
    _L2_gnn_in = {k: v for k, v in _L2_gnn_all.items() if k in ('Wq', 'Wk', 'Wv', 'Wo_w', 'Wo_b', 'ln1_g', 'ln1_b', 'ln2_g', 'ln2_b', 'ffn_w1', 'ffn_b1', 'ffn_w2', 'ffn_b2')}
    del _L2_gnn_all

    def _L3_gnn_setup():
        import jax, jax.numpy as jnp
        import numpy as np
        NEG_SLOPE = 0.2
        key = jax.random.key(seed)
        ks = jax.random.split(key, 8)
        N, E, D, H = (12500, 37500, 256, 256)
        x = jax.random.normal(ks[0], (N, D), dtype=jnp.float32)
        edge_index = jax.random.randint(ks[1], (2, E), 0, N, dtype=jnp.int64)
        s = 0.06
        W = jax.random.normal(ks[2], (H, D), dtype=jnp.float32) * s
        att_src = jax.random.normal(ks[3], (H,), dtype=jnp.float32) * s
        att_dst = jax.random.normal(ks[4], (H,), dtype=jnp.float32) * s
        bias = jnp.zeros((H,), dtype=jnp.float32)
        W_ih = jax.random.normal(ks[5], (4 * H, H), dtype=jnp.float32) * s
        W_hh = jax.random.normal(ks[6], (4 * H, H), dtype=jnp.float32) * s
        return {'x': x, 'edge_index': edge_index, 'W': W, 'att_src': att_src, 'att_dst': att_dst, 'bias': bias, 'W_ih': W_ih, 'W_hh': W_hh}
    _L3_gnn_all = _L3_gnn_setup()
    _L3_gnn_in = {k: v for k, v in _L3_gnn_all.items() if k in ('W', 'att_src', 'att_dst', 'bias', 'W_ih', 'W_hh')}
    del _L3_gnn_all
    return {'x': x, 'src': src, 'dst': dst, 'L0_gnn_W1': _L0_gnn_in['W1'], 'L0_gnn_b1': _L0_gnn_in['b1'], 'L0_gnn_W2': _L0_gnn_in['W2'], 'L0_gnn_b2': _L0_gnn_in['b2'], 'L0_gnn_W3': _L0_gnn_in['W3'], 'L0_gnn_b3': _L0_gnn_in['b3'], 'L0_gnn_W4': _L0_gnn_in['W4'], 'L0_gnn_b4': _L0_gnn_in['b4'], 'L0_gnn_W5': _L0_gnn_in['W5'], 'L0_gnn_b5': _L0_gnn_in['b5'], 'L0_gnn_W6': _L0_gnn_in['W6'], 'L0_gnn_b6': _L0_gnn_in['b6'], 'L1_gnn_W': _L1_gnn_in['W'], 'L1_gnn_b': _L1_gnn_in['b'], 'L2_gnn_Wq': _L2_gnn_in['Wq'], 'L2_gnn_Wk': _L2_gnn_in['Wk'], 'L2_gnn_Wv': _L2_gnn_in['Wv'], 'L2_gnn_Wo_w': _L2_gnn_in['Wo_w'], 'L2_gnn_Wo_b': _L2_gnn_in['Wo_b'], 'L2_gnn_ln1_g': _L2_gnn_in['ln1_g'], 'L2_gnn_ln1_b': _L2_gnn_in['ln1_b'], 'L2_gnn_ln2_g': _L2_gnn_in['ln2_g'], 'L2_gnn_ln2_b': _L2_gnn_in['ln2_b'], 'L2_gnn_ffn_w1': _L2_gnn_in['ffn_w1'], 'L2_gnn_ffn_b1': _L2_gnn_in['ffn_b1'], 'L2_gnn_ffn_w2': _L2_gnn_in['ffn_w2'], 'L2_gnn_ffn_b2': _L2_gnn_in['ffn_b2'], 'L3_gnn_W': _L3_gnn_in['W'], 'L3_gnn_att_src': _L3_gnn_in['att_src'], 'L3_gnn_att_dst': _L3_gnn_in['att_dst'], 'L3_gnn_bias': _L3_gnn_in['bias'], 'L3_gnn_W_ih': _L3_gnn_in['W_ih'], 'L3_gnn_W_hh': _L3_gnn_in['W_hh']}

def reference(x, src, dst, L0_gnn_W1, L0_gnn_b1, L0_gnn_W2, L0_gnn_b2, L0_gnn_W3, L0_gnn_b3, L0_gnn_W4, L0_gnn_b4, L0_gnn_W5, L0_gnn_b5, L0_gnn_W6, L0_gnn_b6, L1_gnn_W, L1_gnn_b, L2_gnn_Wq, L2_gnn_Wk, L2_gnn_Wv, L2_gnn_Wo_w, L2_gnn_Wo_b, L2_gnn_ln1_g, L2_gnn_ln1_b, L2_gnn_ln2_g, L2_gnn_ln2_b, L2_gnn_ffn_w1, L2_gnn_ffn_b1, L2_gnn_ffn_w2, L2_gnn_ffn_b2, L3_gnn_W, L3_gnn_att_src, L3_gnn_att_dst, L3_gnn_bias, L3_gnn_W_ih, L3_gnn_W_hh):
    import jax
    import jax.numpy as jnp

    def _L0_gnn_ref(x, edge_index, W1, b1, W2, b2, W3, b3, W4, b4, W5, b5, W6, b6):
        import jax, jax.numpy as jnp
        import numpy as np
        N_NODES = 6250
        N_EDGES = 100000
        DIMS = [256, 128, 64, 32, 64, 128, 256]

        def _gcn_norm(edge_index, n_nodes):
            loop = jnp.arange(n_nodes, dtype=edge_index.dtype)
            src = jnp.concatenate([edge_index[0], loop])
            dst = jnp.concatenate([edge_index[1], loop])
            deg = jax.ops.segment_sum(jnp.ones_like(dst, dtype=jnp.float32), dst, num_segments=n_nodes)
            dis = jnp.where(deg > 0, jax.lax.rsqrt(jnp.maximum(deg, 1.0)), 0.0)
            norm = dis[src] * dis[dst]
            return (src, dst, norm)

        def _gcn_layer(h, W, b, src, dst, norm, n_nodes):
            h = h @ W
            msg = h[src] * norm[:, None]
            out = jax.ops.segment_sum(msg, dst, num_segments=n_nodes)
            return out + b
        n = x.shape[0]
        src, dst, norm = _gcn_norm(edge_index, n)
        h = jax.nn.relu(_gcn_layer(x, W1, b1, src, dst, norm, n))
        h = jax.nn.relu(_gcn_layer(h, W2, b2, src, dst, norm, n))
        h = _gcn_layer(h, W3, b3, src, dst, norm, n)
        h = jax.nn.relu(_gcn_layer(h, W4, b4, src, dst, norm, n))
        h = jax.nn.relu(_gcn_layer(h, W5, b5, src, dst, norm, n))
        h = _gcn_layer(h, W6, b6, src, dst, norm, n)
        return h

    def _L1_gnn_ref(x, edge_index, W, b):
        import jax, jax.numpy as jnp
        import numpy as np
        N_NODES = 6250
        N_EDGES = 100000
        D_IN = 256
        D_OUT = 256
        N = x.shape[0]
        loop = jnp.arange(N, dtype=edge_index.dtype)
        src = jnp.concatenate([edge_index[0], loop])
        dst = jnp.concatenate([edge_index[1], loop])
        deg = jax.ops.segment_sum(jnp.ones_like(src, dtype=x.dtype), dst, num_segments=N)
        deg_inv_sqrt = jnp.where(deg > 0, jax.lax.rsqrt(jnp.maximum(deg, 1.0)), 0.0)
        norm = deg_inv_sqrt[src] * deg_inv_sqrt[dst]
        h = jnp.einsum('nd,od->no', x, W)
        msg = h[src] * norm[:, None]
        out = jax.ops.segment_sum(msg, dst, num_segments=N) + b
        return jax.nn.relu(out)

    def _L2_gnn_ref(x, edge_index, batch, Wq, Wk, Wv, Wo_w, Wo_b, ln1_g, ln1_b, ln2_g, ln2_b, ffn_w1, ffn_b1, ffn_w2, ffn_b2):
        import jax, jax.numpy as jnp
        import numpy as np
        N, E = (6250, 100000)
        IN_DIM = 256
        OUT_DIM = 256
        H = 8
        D = OUT_DIM // H
        SCALE = D ** (-0.5)
        LN_EPS = 1e-05

        def _layernorm(x, g, b):
            mu = jnp.mean(x, axis=-1, keepdims=True)
            var = jnp.mean((x - mu) ** 2, axis=-1, keepdims=True)
            return (x - mu) * jax.lax.rsqrt(var + LN_EPS) * g + b
        n = x.shape[0]
        residual = x
        Q = (x @ Wq).reshape(n, H, D)
        K = (x @ Wk).reshape(n, H, D)
        V = (x @ Wv).reshape(n, H, D)
        src, dst = (edge_index[0], edge_index[1])
        scores = jnp.einsum('ehd,ehd->eh', Q[dst], K[src]) * SCALE
        attn_max = jnp.zeros((n, H), scores.dtype).at[dst].max(scores)
        w = jnp.exp(scores - attn_max[dst])
        attn_sum = jnp.zeros((n, H), w.dtype).at[dst].add(w)
        w = w / (attn_sum[dst] + 1e-08)
        msg = V[src] * w[:, :, None]
        out = jnp.zeros((n, H, D), msg.dtype).at[dst].add(msg)
        out = out.reshape(n, OUT_DIM) @ Wo_w + Wo_b
        out = _layernorm(residual + out, ln1_g, ln1_b)
        ffn = jax.nn.gelu(out @ ffn_w1 + ffn_b1, approximate=False) @ ffn_w2 + ffn_b2
        out = _layernorm(out + ffn, ln2_g, ln2_b)
        return out

    def _L3_gnn_ref(x, edge_index, W, att_src, att_dst, bias, W_ih, W_hh):
        import jax, jax.numpy as jnp
        import numpy as np
        NEG_SLOPE = 0.2
        N = x.shape[0]
        loops = jnp.arange(N, dtype=edge_index.dtype)
        src = jnp.concatenate([edge_index[0], loops])
        dst = jnp.concatenate([edge_index[1], loops])
        xp = x @ W.T
        a_src = xp @ att_src
        a_dst = xp @ att_dst
        e = jax.nn.leaky_relu(a_src[src] + a_dst[dst], NEG_SLOPE)
        emax = jax.ops.segment_max(e, dst, num_segments=N)
        ex = jnp.exp(e - emax[dst])
        denom = jax.ops.segment_sum(ex, dst, num_segments=N)
        alpha = ex / denom[dst]
        agg = jax.ops.segment_sum(alpha[:, None] * xp[src], dst, num_segments=N)
        hb = jnp.tanh(agg + bias)
        h0 = jnp.zeros_like(hb)
        gates = hb @ W_ih.T + h0 @ W_hh.T
        i, f, g, o = jnp.split(gates, 4, axis=-1)
        c1 = jax.nn.sigmoid(i) * jnp.tanh(g)
        h1 = jax.nn.sigmoid(o) * jnp.tanh(c1)
        return h1
    edge_index = jnp.stack([src, dst])
    batch0 = jnp.zeros((6250,), jnp.int32)
    x = _layernorm(x + _L0_gnn_ref(x, edge_index, L0_gnn_W1, L0_gnn_b1, L0_gnn_W2, L0_gnn_b2, L0_gnn_W3, L0_gnn_b3, L0_gnn_W4, L0_gnn_b4, L0_gnn_W5, L0_gnn_b5, L0_gnn_W6, L0_gnn_b6), axis=-1)
    x = _layernorm(x + _L1_gnn_ref(x, edge_index, L1_gnn_W, L1_gnn_b), axis=-1)
    x = _layernorm(x + _L2_gnn_ref(x, edge_index, batch0, L2_gnn_Wq, L2_gnn_Wk, L2_gnn_Wv, L2_gnn_Wo_w, L2_gnn_Wo_b, L2_gnn_ln1_g, L2_gnn_ln1_b, L2_gnn_ln2_g, L2_gnn_ln2_b, L2_gnn_ffn_w1, L2_gnn_ffn_b1, L2_gnn_ffn_w2, L2_gnn_ffn_b2), axis=-1)
    x = _layernorm(x + _L3_gnn_ref(x, edge_index, L3_gnn_W, L3_gnn_att_src, L3_gnn_att_dst, L3_gnn_bias, L3_gnn_W_ih, L3_gnn_W_hh), axis=-1)
    return x

_drawn_inputs = setup_inputs


def setup_inputs(seed=0):
    import zlib

    import numpy as np

    out = dict(_drawn_inputs(seed))
    spreads = {'L0_gnn_b1': (0.0, 0.289),
     'L0_gnn_b2': (0.0, 0.283),
     'L0_gnn_b3': (0.0, 0.1),
     'L0_gnn_b4': (0.0, 0.1),
     'L0_gnn_b5': (0.0, 0.1),
     'L0_gnn_b6': (0.0, 0.1),
     'L1_gnn_b': (0.0, 0.1),
     'L2_gnn_Wo_b': (0.0, 0.1),
     'L2_gnn_ln1_g': (1.0, 0.2),
     'L2_gnn_ln1_b': (0.0, 0.1),
     'L2_gnn_ln2_g': (1.0, 0.2),
     'L2_gnn_ln2_b': (0.0, 0.1),
     'L2_gnn_ffn_b1': (0.0, 0.337),
     'L2_gnn_ffn_b2': (0.0, 0.1),
     'L3_gnn_bias': (0.0, 0.397)}
    factors = {'L0_gnn_W1': 8.0,
     'L2_gnn_Wq': 3.482,
     'L2_gnn_Wk': 3.457,
     'L3_gnn_att_dst': 23.371,
     'L3_gnn_att_src': 2.858}
    for name, (base, spread) in spreads.items():
        noise = np.random.default_rng([zlib.crc32(name.encode()), seed]).standard_normal(out[name].shape)
        drawn = base * np.exp(spread * noise) if base else spread * noise
        out[name] = jnp.asarray(drawn.astype(out[name].dtype))
    for name, factor in factors.items():
        out[name] = (out[name] * factor).astype(out[name].dtype)
    return out
```

```python
from contextlib import ExitStack

import concourse.bass as bass
from concourse import mybir

F32 = mybir.dt.float32
I32 = mybir.dt.int32
BF16 = mybir.dt.bfloat16
ALU = mybir.AluOpType
ACT = mybir.ActivationFunctionType
AX = mybir.AxisListType
DVE = mybir.EngineType.DVE
PE = mybir.EngineType.PE
ds = bass.ds

P = 128
N = 6250
E = 100000
D = 256
TILES = -(-N // P)
TP = TILES + TILES % 2
NP = TP * P
CHUNKS = -(-E // P)
U = 16
HALF = U // 2
TURNS = -(-(CHUNKS + TILES - 1) // U)
VISITS = TURNS * U
VT = -(-(VISITS + U) // P) * P
VB = VT // P
CROWS = CHUNKS + 2
NO_NODE = 1 << 20
HEADS = 8
HD = D // HEADS
EC, EP = 800, 125
SUM_BANKS = 4
SBANK = 4
BIAS_W = {"L0_gnn_b1": 128, "L0_gnn_b2": 64, "L0_gnn_b3": 32, "L0_gnn_b4": 64, "L0_gnn_b5": 128,
          "L0_gnn_b6": 256, "L1_gnn_b": 256, "L2_gnn_Wo_b": 256, "L2_gnn_ln1_g": 256, "L2_gnn_ln1_b": 256,
          "L2_gnn_ln2_g": 256, "L2_gnn_ln2_b": 256, "L2_gnn_ffn_b2": 256, "L3_gnn_bias": 256}
EPS = 1e-5


class Steps:

    def __init__(self, eng, sem):
        self.eng, self.sem, self.base, self.n, self.i, self.per = eng, sem, 0, 0, None, 0

    def link(self, ins):
        ins.then_inc(self.sem, 1)
        self.n += 1
        self.eng.wait_ge(self.sem, self.base + self.n if self.i is None else self.i * self.per + (self.base + self.n))

    def enter(self, i, per):
        self.base += self.n
        self.i, self.per, self.n = i, per, 0

    def leave(self, turns):
        assert self.n == self.per, (self.n, self.per)
        self.base += self.per * turns
        self.n, self.i = 0, None


def build_program(nc, a, out, last_stage=99):
    ctx = ExitStack()
    with ctx:
        def sb(name, shape, dt=F32):
            return ctx.enter_context(nc.sbuf_tensor(name, shape, dt))

        def sem(name):
            return ctx.enter_context(nc.semaphore(name))

        X = sb("X", [P, TP * D])
        ACC = sb("ACC", [P, TP * (D + HEADS)])
        S = sb("S", [P, (VISITS + HALF) * HEADS])
        ring = sb("ring", [P, U, D + HEADS])
        idx_tab = sb("idx_tab", [P, VT], I32)
        idx_now = sb("idx_now", [P, U], I32)
        dloc = sb("dloc", [P, VT])
        dlast = sb("dlast", [P, VT])
        tile_of = sb("tile_of", [1, VT], I32)
        dis = sb("dis", [P, TP])
        onehot = sb("onehot", [P, U, P])
        iota = sb("iota", [P, P])
        ident = sb("ident", [P, P + 1])
        ones = sb("ones", [P, P])
        onehotT = sb("onehotT", [P, 2, HALF, P])
        message = sb("message", [P, 4, D])
        early = message[:, :, :].rearrange("p u d -> p (u d)")
        W1 = early[:, 0:256].rearrange("p (k n) -> p k n", k=2)
        W6 = early[:, 256:512]
        early_bias = {"L0_gnn_b1": early[:, 512:640], "L0_gnn_b5": early[:, 640:768], "L0_gnn_b6": early[:, 768:1024]}
        bias = {n: early_bias[n] if n in early_bias else sb("bc_" + n, [P, w]) for n, w in BIAS_W.items()}
        Wqkv = S[:, 1100:1100 + 6 * D].rearrange("p (w k n) -> p w k n", w=3, k=2)
        weight = sb("weight", [P, 2, HALF])
        minus = sb("minus", [P, 2, HALF * HEADS])
        node_max = sb("node_max", [P, TP * HEADS])
        node_src = sb("node_src", [P, TP])
        node_e = sb("node_e", [P, TP, 2])
        src_now = sb("src_now", [P, U])
        small = sb("small", [P, 64])
        moments = sb("moments", [P, TP, 6])
        mean = sb("mean", [P, TP])
        rstd = sb("rstd", [P, TP])
        tmp2 = sb("tmp2", [P, TP])
        shift = sb("shift", [P, TP])
        root = sb("root", [P, TP])
        W2 = sb("W2", [128, 64])
        W3 = sb("W3", [64, 32])
        W4 = sb("W4", [32, 64])
        W5 = sb("W5", [64, 128])
        L1T = sb("L1T", [P, 2, D])
        L3T = sb("L3T", [P, 2, D + 2])
        WihT = sb("WihT", [P, 2, 3 * D])
        Wo = sb("Wo", [P, 2, D])
        fb1 = sb("fb1", [P, 4])

        def accv(lo, n, dt=F32, p=P):
            v = ACC[0:p, lo:lo + n]
            return v if dt == F32 else v.bitcast(dt)

        dst_i = accv(0, EC, I32, EP)
        hi_i = accv(800, EC, I32, EP)
        lo_i = accv(1600, EC, I32, EP)
        hi_f = accv(2400, EC, F32, EP)
        lo_f = accv(3200, EC, F32, EP)
        edge_i = accv(4000, VB * 2 * P, I32).rearrange("p (k w) -> p k w", k=VB)
        edge_f = accv(5800, VB * 2 * P).rearrange("p (k w) -> p k w", k=VB)
        passed = accv(7600, VT, F32, TILES - 1)
        viota = accv(8500, VT)
        tri = accv(9400, P)
        hist = accv(9530, P, F32, TILES)
        dnext = accv(9700, VT)
        viota_i = accv(10600, VT, I32)
        hi_i_rows = accv(11500, VT, I32).rearrange("p (k e) -> p k e", k=VB)
        hi_b_rows = accv(12400, VT // 2).bitcast(BF16).rearrange("p (k e) -> p k e", k=VB)
        nat_L1 = S[:, 0:512].rearrange("p (o d) -> p o d", o=2)
        nat_L3 = S[:, 512:1024].rearrange("p (o d) -> p o d", o=2)
        nat_ih = S[:, 1024:2560].rearrange("p (o d) -> p o d", o=6)
        att = S[:, 2560:2564]
        oh_lo = S[0:EP, 2600:2600 + 2048].bitcast(BF16).rearrange("p (b c n) -> p b c n", b=2, c=U)
        oh_hi = S[0:EP, 4700:4700 + U * TILES].bitcast(BF16).rearrange("p (b c n) -> p b c n", b=2, c=U)
        fw1 = S[:, 0:1024].rearrange("p (k n) -> p k n", k=2)
        fw2 = S[:, 1024:2048].rearrange("p (k n) -> p k n", k=4)
        asrc = S[:, 2048:2048 + VT]
        asrc_up = S[:, 3072:3072 + VT]
        run_src = S[:, 4096:4096 + VT]
        node_self = S[:, 5000:5000 + TP]
        src_rows = S[0:TP, 5100:5100 + P]
        src_hi = S[0:TP, 0:U * P].bitcast(BF16).rearrange("p (b e) -> p b e", b=2)
        src_lo = S[:, 5240:5240 + VT]
        iota_b = S[:, 5600:5664].bitcast(BF16)
        zero_b = S[:, 5700:5764].bitcast(BF16)
        pad_i = S[0:2, 5800:5800 + 2 * P].bitcast(I32)

        ringf = ring[:, :, :].rearrange("p u d -> p (u d)")
        turned = ringf[:, 0:512].rearrange("p (b k n) -> p b k n", b=2, k=2)
        pre = ringf[:, 1024:1536].rearrange("p (b n) -> p b n", b=2)
        hidden = ringf[:, 2048:3072].rearrange("p (b f n) -> p b f n", b=2, f=4)
        gates = ringf[:, 2048:3584].rearrange("p (b g n) -> p b g n", b=2, g=3)
        tile_onehot = ringf[0:TP, 0:2 * U * P].rearrange("p (b e) -> p b e", b=2)
        st_s = ringf[:, 0:512]
        st_d = ringf[:, 512:1024]
        run = ringf[:, 1024:1536]
        run_tmp = ringf[:, 1536:2048]
        run_dst = ringf[:, 2048:2560]
        mid = ringf[:, 1536:2048].rearrange("p (b n) -> p b n", b=2)

        bank = [ctx.enter_context(nc.psum_tensor(f"bank{i}", [P, 512], F32)) for i in range(8)]

        edges_d = nc.dram_tensor("edges_d", (CROWS, 2 * P), I32).ap()
        widths = [128, 64, 32, 32, 64, 128, 256]
        tables = [nc.dram_tensor(f"table{p}", (NP, w), F32).ap() for p, w in enumerate(widths)]
        k_table = nc.dram_tensor("k_table", (NP, D), F32).ap()
        v_table = nc.dram_tensor("v_table", (NP, D), F32).ap()
        xp_table = nc.dram_tensor("xp_table", (NP, D), F32).ap()
        hi_rows = nc.dram_tensor("hi_rows", (VT, P), BF16).ap()
        AW = D + HEADS
        GW = D + 1
        accoff = [0, 0, 0, 0, 1600, 4800, 0]

        def acc_tile(p, t):
            return ACC[:, ds(t * widths[p] + accoff[p], widths[p])]

        x_in = sem("x_in")
        pads_set = sem("pads_set")
        edges_in = sem("edges_in")
        edges_padded = sem("edges_padded")
        dst_in = sem("dst_in")
        weights_in = sem("weights_in")
        natural_in = sem("natural_in")
        bias_in = sem("bias_in")
        consts_set = sem("consts_set")
        x_tail_set = sem("x_tail_set")
        weight_turned = sem("weight_turned")
        weight_copied = sem("weight_copied")
        oh_built = sem("oh_built")
        oh_counted = sem("oh_counted")
        setup_pe = sem("setup_pe")
        setup_dve = sem("setup_dve")
        rows_of_chunk = sem("rows_of_chunk")
        vec = sem("vec")
        rows_in = [sem(f"rows_in{j}") for j in range(U)]
        idx_copied = sem("idx_copied")
        onehot_ready = sem("onehot_ready")
        sums_ready = sem("sums_ready")
        sums_added = sem("sums_added")
        rows_used = sem("rows_used")
        table_out = sem("table_out")
        root_asked = sem("root_asked")
        root_taken = sem("root_taken")
        x_ready = sem("x_ready")
        tail_set = sem("tail_set")
        kv_out = sem("kv_out")
        qkv_in = sem("qkv_in")
        kv_ready = sem("kv_ready")
        ot_turned = sem("ot_turned")
        ot_copied = sem("ot_copied")
        scores_done = sem("scores_done")
        hs_s = sem("hs_s")
        hs_d = sem("hs_d")
        hs_turned = sem("hs_turned")
        hs_run = sem("hs_run")
        hs_done = sem("hs_done")
        hs_back = sem("hs_back")
        hs_out = sem("hs_out")
        sweep_ready = sem("sweep_ready")
        sweep_max = sem("sweep_max")
        expand_ready = sem("expand_ready")
        weights_minus = sem("weights_minus")
        weights_ready = sem("weights_ready")
        acc_zero = sem("acc_zero")
        parts_set = sem("parts_set")
        parts_joined = sem("parts_joined")
        ffn_in = sem("ffn_in")
        h_product = sem("h_product")
        h_done = sem("h_done")
        y_ready = sem("y_ready")
        src_turned = sem("src_turned")
        src_rows_ready = sem("src_rows_ready")
        hi_rows_set = sem("hi_rows_set")
        hi_rows_out = sem("hi_rows_out")
        hi_in = [sem(f"hi_in{b}") for b in range(2)]
        tile_onehot_built = sem("tile_onehot_built")
        row_looked_up = sem("row_looked_up")
        src_taken = sem("src_taken")
        tile_onehots_asked = sem("tile_onehots_asked")
        xp_out = sem("xp_out")
        src_copied = sem("src_copied")
        src_up = sem("src_up")
        least_step = sem("least_step")
        least_turned = sem("least_turned")
        self_ready = sem("self_ready")
        scaled_ready = sem("scaled_ready")
        gates_ready = sem("gates_ready")
        cell_ready = sem("cell_ready")
        cell_tanh = sem("cell_tanh")
        gathers_asked = sem("gathers_asked")
        transposes_asked = sem("transposes_asked")
        d_pre = sem("d_pre")
        d_turned = sem("d_turned")
        d_evac = sem("d_evac")
        d_product = sem("d_product")
        d_post = sem("d_post")
        pass_init = sem("pass_init")
        out_done = sem("out_done")

        block = ctx.enter_context(nc.Block())

        n_weights = [0]

        def setup_sync(sp):
            sp.dma_start(dst_i, a["dst"].rearrange("(p c) -> p c", p=EP)).then_inc(dst_in, 16)
            full = (CHUNKS - 1) * P
            for k, name in enumerate(("src", "dst")):
                sp.dma_start(edges_d[0:CHUNKS - 1, k * P:(k + 1) * P],
                             a[name][0:full].rearrange("(c e) -> c e", e=P)).then_inc(edges_in, 16)
                sp.dma_start(edges_d[CHUNKS - 1:CHUNKS, k * P:k * P + E - full],
                             a[name][full:E].rearrange("(c e) -> c e", c=1)).then_inc(edges_in, 16)
            for o, name in enumerate(("L1_gnn_W", "L3_gnn_W")):
                sp.dma_start((nat_L1, nat_L3)[o], a[name].rearrange("(o p) d -> p o d", p=P)).then_inc(natural_in, 16)
            for g, row in enumerate((0, 2 * D, 3 * D)):
                sp.dma_start(nat_ih[:, 2 * g:2 * g + 2, :],
                             a["L3_gnn_W_ih"][row:row + D, :].rearrange("(o p) d -> p o d", p=P)).then_inc(natural_in, 16)
            for k, name in enumerate(("L3_gnn_att_src", "L3_gnn_att_dst")):
                sp.dma_start(att[:, 2 * k:2 * k + 2], a[name].rearrange("(o p) -> p o", p=P),
                             allow_slow_non_contiguous=True).then_inc(natural_in, 16)
            full_t = N // P
            sp.dma_start(X[:, 0:full_t * D].rearrange("p (t d) -> p t d", d=D),
                         a["x"][0:full_t * P, :].rearrange("(t p) d -> p t d", p=P)).then_inc(x_in, 16)
            loads = [(W1, a["L0_gnn_W1"].rearrange("(k p) n -> p k n", p=P)),
                     (W2[:, :], a["L0_gnn_W2"]), (W3[:, :], a["L0_gnn_W3"]), (W4[:, :], a["L0_gnn_W4"]),
                     (W5[:, :], a["L0_gnn_W5"]), (W6, a["L0_gnn_W6"]),
                     (Wo[:, :, :], a["L2_gnn_Wo_w"].rearrange("(k p) n -> p k n", p=P)),
                     (fb1[:, :], a["L2_gnn_ffn_b1"].rearrange("(f p) -> p f", p=P))]
            for dst, src in loads:
                sp.dma_start(dst, src, allow_slow_non_contiguous=True).then_inc(weights_in, 16)
            for name, w in BIAS_W.items():
                sp.dma_start(bias[name][:, :], a[name].rearrange("(o d) -> o d", o=1).to_broadcast([P, w])
                             ).then_inc(bias_in, 16)
            sp.wait_ge(x_tail_set, 1)
            sp.dma_start(X[0:N - full_t * P, full_t * D:(full_t + 1) * D], a["x"][full_t * P:N, :]).then_inc(x_in, 16)
            sp.wait_ge(pads_set, 2)
            sp.dma_start(edges_d[CHUNKS - 1:CHUNKS, E - full:P], pad_i[0:1, E - full:P]).then_inc(edges_padded, 16)
            sp.dma_start(edges_d[CHUNKS - 1:CHUNKS, P + E - full:2 * P], pad_i[0:1, P + E - full:2 * P]).then_inc(edges_padded, 16)
            sp.dma_start(edges_d[CHUNKS:CROWS, :], pad_i).then_inc(edges_padded, 16)
            sp.wait_ge(hi_rows_set, 1)
            sp.dma_start(hi_rows.rearrange("(k p) e -> p k e", p=P), hi_b_rows).then_inc(hi_rows_out, 16)
            sp.wait_ge(hi_rows_out, 16)

        def setup_pool(pool):
            pool.memset(X[:, (TILES - 1) * D:TP * D], 0.0).then_inc(x_tail_set, 1)
            pool.memset(pad_i[:, 0:P], 0).then_inc(pads_set, 1)
            pool.memset(pad_i[:, P:2 * P], NO_NODE).then_inc(pads_set, 1)
            pool.iota(viota_i, [[1, VT]], base=0, channel_multiplier=0).then_inc(consts_set, 1)
            pool.iota(small[:, 0:VB].bitcast(I32), [[P, VB]], base=0, channel_multiplier=1).then_inc(consts_set, 1)
            pool.iota(small[:, 16:17].bitcast(I32), [[1, 1]], base=0, channel_multiplier=1).then_inc(consts_set, 1)
            pool.memset(ident[:, :], 0.0).then_inc(consts_set, 1)
            pool.memset(ones[:, :], 1.0).then_inc(consts_set, 1)
            pool.memset(zero_b, 0.0).then_inc(consts_set, 1)
            pool.wait_ge(consts_set, 6)
            pool.affine_select(out=ident[:, :], in_=ident[:, :], compare_op=ALU.not_equal, fill=1.0, base=0,
                               pattern=[[-1, P + 1]], channel_multiplier=1).then_inc(consts_set, 1)
            pool.affine_select(out=tri, in_=ones[:, :], compare_op=ALU.is_ge, fill=0.0, base=0,
                               pattern=[[1, P]], channel_multiplier=-1).then_inc(consts_set, 1)
            pool.wait_ge(edges_in, 64)
            pool.wait_ge(edges_padded, 48)
            pool.wait_ge(setup_dve, 5)
            for k in range(VB):
                nc.gpsimd.indirect_dma_start(edge_i[:, k, :], None, edges_d,
                                             bass.IndirectOffsetOnAxis(small[:, 48 + k:49 + k].bitcast(I32), 0)
                                             ).then_inc(rows_of_chunk, 16)

        nat_blocks = ([(L1T[:, db, ob * P:(ob + 1) * P], nat_L1[:, ob, db * P:(db + 1) * P]) for db in range(2) for ob in range(2)]
                      + [(L3T[:, db, ob * P:(ob + 1) * P], nat_L3[:, ob, db * P:(db + 1) * P]) for db in range(2) for ob in range(2)]
                      + [(WihT[:, db, ob * P:(ob + 1) * P], nat_ih[:, ob, db * P:(db + 1) * P]) for db in range(2) for ob in range(6)])

        def setup_tensor(pe):
            pe.sem_inc(sums_ready, U)
            pe.sem_inc(oh_counted, 2)
            pe.sem_inc(d_turned, 2)
            pe.sem_inc(d_product, 2)
            pe.sem_inc(hs_turned, 1)
            pe.wait_ge(consts_set, 8)
            pe.wait_ge(natural_in, 16 * 7)
            for n, (_, src) in enumerate(nat_blocks):
                if n >= 2:
                    pe.wait_ge(weight_copied, n - 1)
                pe.transpose(bank[n % 2][:, 0:P], src, ident[:, 0:P]).then_inc(weight_turned, 1)
            for db in range(2):
                for k in range(2):
                    for ob in range(2):
                        m = pe.matmul(bank[2][:, 2 * db + k:2 * db + k + 1], nat_L3[:, ob, db * P:(db + 1) * P],
                                      att[:, 2 * k + ob:2 * k + ob + 1], start=(ob == 0), stop=(ob == 1))
            m.then_inc(weight_turned, 1)
            pe.matmul(bank[3][0:TILES, 0:P], zero_b[:, 0:TILES], zero_b, start=True, stop=False, skip_group_check=True)
            with pe.Fori(0, EC // U // 2) as i:
                for b in range(2):
                    pe.wait_ge(oh_built, i * 4 + 2 * b + 2)
                    for c in range(U):
                        m = pe.matmul(bank[3][0:TILES, 0:P], oh_hi[:, b, c, :], oh_lo[:, b, c, :], start=False, stop=False,
                                      skip_group_check=True)
                    m.then_inc(oh_counted, 1)
            pe.matmul(bank[3][0:TILES, 0:P], zero_b[:, 0:TILES], zero_b, start=False, stop=True,
                      skip_group_check=True).then_inc(setup_pe, 1)
            pe.wait_ge(setup_dve, 2)
            pe.transpose(bank[4][:, 0:TILES], hist, ident[0:TILES, 0:TILES]).then_inc(setup_pe, 1)
            pe.matmul(bank[5][0:TILES - 1, 0:1], tri[0:TILES, 0:TILES - 1], small[0:TILES, 20:21], start=True,
                      stop=True).then_inc(setup_pe, 1)
            pe.wait_ge(setup_dve, 4)
            for k in range(VB):
                m = pe.matmul(bank[6][:, k:k + 1], passed[:, k * P:(k + 1) * P], ones[0:TILES - 1, 0:1], start=True, stop=True)
            m.then_inc(setup_pe, 1)
            for k in range(2):
                m = pe.matmul(bank[4 + k][:, 0:VT // 2], ones[0:TILES - 1, :], passed[:, k * (VT // 2):(k + 1) * (VT // 2)],
                              start=True, stop=True)
            m.then_inc(setup_pe, 1)
            pe.wait_ge(setup_dve, 6)
            for k in range(VB):
                for s in range(2):
                    b = 2 * (k % 2) + s
                    if k >= 2:
                        pe.wait_ge(setup_dve, 7 + 2 * (k - 2) + s)
                    elif k == 1 and s == 1:
                        pass
                    pe.transpose(bank[b][:, 0:P], edge_f[:, k, s * P:(s + 1) * P], ident[:, 0:P]).then_inc(setup_pe, 1)
            pe.wait_ge(setup_dve, 6 + 2 * VB)
            for k in range(2):
                m = pe.matmul(bank[4 + k][:, 0:VT // 2], ident[:, 1:P + 1], dloc[:, k * (VT // 2):(k + 1) * (VT // 2)],
                              start=True, stop=True)
            m.then_inc(setup_pe, 1)

        def setup_scalar(act):
            act.sem_inc(d_evac, 2)
            act.sem_inc(ot_copied, 2)
            act.sem_inc(src_copied, 2)
            for n, (dst, _) in enumerate(nat_blocks):
                act.wait_ge(weight_turned, n + 1)
                act.copy(dst, bank[n % 2][:, 0:P]).then_inc(weight_copied, 1)
            act.wait_ge(weight_turned, len(nat_blocks) + 1)
            act.copy(L3T[:, :, D:D + 2], bank[2][:, 0:4].rearrange("p (b k) -> p b k", b=2)).then_inc(weight_copied, 1)

        roots = [0, 0]

        def inverse_root(v, st, x, tmp, n):
            y = tmp2[:, 0:n]
            v.sem_inc(root_asked, 1)
            roots[0] += 1
            v.wait_ge(root_taken, roots[0])
            st.link(v.reciprocal(tmp, tmp))
            st.link(v.tensor_tensor(y, tmp, tmp, ALU.mult))
            st.link(v.tensor_tensor(y, y, x, ALU.mult))
            st.link(v.tensor_scalar(y, y, -0.5, 1.5, ALU.mult, ALU.add))
            st.link(v.tensor_tensor(x, y, tmp, ALU.mult))

        def take_root(act, x, tmp):
            roots[1] += 1
            act.wait_ge(root_asked, roots[1])
            act.activation(tmp, x, ACT.Sqrt).then_inc(root_taken, 1)

        def setup_vector(v, st):
            v.sem_inc(sums_added, SUM_BANKS)
            v.sem_inc(rows_used, U)
            v.sem_inc(d_post, 2)
            v.sem_inc(sweep_max, U)
            v.sem_inc(weights_minus, 2)
            v.memset(S[:, VISITS * HEADS:], 0.0).then_inc(tail_set, 1)
            v.wait_ge(consts_set, 8)
            st.link(v.tensor_copy(viota, viota_i))
            st.link(v.tensor_copy(small[:, 8:8 + VB], small[:, 0:VB].bitcast(I32)))
            st.link(v.tensor_copy(small[:, 17:18], small[:, 16:17].bitcast(I32)))
            st.link(v.tensor_copy(iota[:, :], viota[:, 0:P]))
            st.link(v.tensor_copy(iota_b, iota[:, :]))
            v.wait_ge(dst_in, 16)
            st.link(v.tensor_scalar(hi_i, dst_i, 7, None, ALU.arith_shift_right))
            st.link(v.tensor_scalar(lo_i, dst_i, P - 1, None, ALU.bitwise_and))
            st.link(v.tensor_copy(hi_f, hi_i))
            st.link(v.tensor_copy(lo_f, lo_i))
            with v.Fori(0, EC // U // 2) as i:
                for b in range(2):
                    v.wait_ge(oh_counted, i * 2 + (b + 1))
                    v.tensor_tensor(oh_lo[:, b], iota_b[0:EP, :].unsqueeze(1).to_broadcast([EP, U, P]),
                                    lo_f[:, ds(i * (2 * U) + b * U, U)].unsqueeze(2).to_broadcast([EP, U, P]),
                                    ALU.is_equal).then_inc(oh_built, 1)
                    v.tensor_tensor(oh_hi[:, b], iota_b[0:EP, 0:TILES].unsqueeze(1).to_broadcast([EP, U, TILES]),
                                    hi_f[:, ds(i * (2 * U) + b * U, U)].unsqueeze(2).to_broadcast([EP, U, TILES]),
                                    ALU.is_equal).then_inc(oh_built, 1)
            v.wait_ge(setup_pe, 1)
            v.tensor_copy(hist, bank[3][0:TILES, 0:P]).then_inc(setup_dve, 1)
            v.wait_ge(setup_dve, 1)
            v.tensor_reduce(small[0:TILES, 20:21], hist, AX.X, ALU.add).then_inc(setup_dve, 1)
            v.wait_ge(setup_pe, 2)
            st.link(v.memset(dis[:, :], 1.0))
            st.link(v.tensor_scalar(dis[:, 0:TILES], bank[4][:, 0:TILES], 1.0, None, ALU.add))
            inverse_root(v, st, dis[:, 0:TILES], root[:, 0:TILES], TILES)
            v.wait_ge(setup_pe, 3)
            pos = small[0:TILES - 1, 21:22].bitcast(I32)
            st.link(v.tensor_copy(pos, bank[5][0:TILES - 1, 0:1]))
            st.link(v.tensor_scalar(small[0:TILES - 1, 22:23].bitcast(I32), pos, 7, None, ALU.arith_shift_right))
            st.link(v.tensor_copy(small[0:TILES - 1, 23:24], small[0:TILES - 1, 22:23].bitcast(I32)))
            v.tensor_tensor(small[0:TILES - 1, 24:25], small[0:TILES - 1, 23:24], small[0:TILES - 1, 17:18],
                            ALU.add).then_inc(setup_dve, 1)
            v.wait_ge(setup_dve, 3)
            v.tensor_scalar(passed, viota[0:TILES - 1, :], small[0:TILES - 1, 24:25], None, ALU.is_gt).then_inc(setup_dve, 1)
            v.wait_ge(setup_pe, 4)
            st.link(v.tensor_tensor(small[:, 32:32 + VB], small[:, 8:8 + VB], bank[6][:, 0:VB], ALU.subtract))
            v.tensor_scalar(small[:, 48:48 + VB].bitcast(I32), small[:, 32:32 + VB], float(CROWS - 1), None,
                            ALU.min).then_inc(setup_dve, 1)
            v.wait_ge(setup_pe, 5)
            h = VT // 2
            for k in range(2):
                st.link(v.tensor_copy(tile_of[:, k * h:(k + 1) * h], bank[4 + k][0:1, 0:h]))
            for k in range(2):
                st.link(v.tensor_scalar(dnext[:, k * h:(k + 1) * h], bank[4 + k][:, 0:h], float(P), None, ALU.mult))
            v.wait_ge(rows_of_chunk, 16 * VB)
            v.tensor_copy(edge_f, edge_i).then_inc(setup_dve, 1)
            st.link(v.tensor_scalar(hi_i_rows, edge_i[:, :, 0:P], 7, None, ALU.arith_shift_right))
            v.tensor_copy(hi_b_rows, hi_i_rows).then_inc(hi_rows_set, 1)
            for k in range(VB):
                v.wait_ge(setup_pe, 5 + 2 * k + 1)
                v.tensor_copy(idx_tab[:, k * P:(k + 1) * P], bank[2 * (k % 2)][:, 0:P]).then_inc(setup_dve, 1)
                v.wait_ge(setup_pe, 5 + 2 * k + 2)
                v.tensor_tensor(dloc[:, k * P:(k + 1) * P], bank[2 * (k % 2) + 1][:, 0:P], dnext[:, k * P:(k + 1) * P],
                                ALU.subtract).then_inc(setup_dve, 1)
            v.wait_ge(setup_dve, 6 + 2 * VB)
            v.wait_ge(setup_pe, 6 + 2 * VB)
            st.link(v.tensor_scalar(small[:, 25:26], small[:, 17:18], float(P - 1), None, ALU.is_equal))
            for k in range(2):
                st.link(v.tensor_tensor(dnext[:, k * h:(k + 1) * h], bank[4 + k][:, 0:h], dloc[:, k * h:(k + 1) * h],
                                        ALU.not_equal))
            st.link(v.tensor_scalar(dnext, dnext, small[:, 25:26], None, ALU.max))
            st.link(v.tensor_scalar(dlast[:, :], dloc[:, :], 1.0, None, ALU.add))
            st.link(v.tensor_tensor(dlast[:, :], dlast[:, :], dnext, ALU.mult))
            st.link(v.tensor_scalar(dlast[:, :], dlast[:, :], -1.0, None, ALU.add))

        def gather_rows(pool, g, table, w, used, base, stored, stored_sem=table_out):
            with pool.Fori(0, TURNS) as i:
                for h in range(2):
                    pool.wait_ge(used, i * U + (base + h * HALF + HALF))
                    pool.tensor_copy(idx_now[:, h * HALF:(h + 1) * HALF],
                                     idx_tab[:, ds(i * U + h * HALF, HALF)]).then_inc(idx_copied, 1)
                    pool.wait_ge(idx_copied, i * 2 + (g * 2 * TURNS + h + 1))
                    pool.wait_ge(stored_sem, stored)
                    pool.sem_inc(gathers_asked, 1)
                    for j in range(h * HALF, (h + 1) * HALF):
                        nc.gpsimd.indirect_dma_start(ring[:, j, 0:w], None, table,
                                                     bass.IndirectOffsetOnAxis(idx_now[:, j:j + 1], 0)
                                                     ).then_inc(rows_in[j], 16)

        def load_tiles(eng, regs, i, lo, n):
            eng.load(regs[0:n], tile_of[0:1, ds(i * U + lo, n)])
            return [eng.snap(r, min_val=0, max_val=TILES - 1) for r in regs[0:n]]

        def sum_tensor(pe, p, g, m, oh_base):
            w = widths[p]
            with pe.Fori(0, TURNS) as i:
                for j in range(U):
                    pe.wait_ge(rows_in[j], i * 16 + 16 * (g * TURNS + 1))
                    pe.wait_ge(onehot_ready, i * U + (oh_base + j + 1))
                    pe.wait_ge(sums_added, i * U + (m * VISITS + j + 1))
                    pe.matmul(bank[SBANK + j % SUM_BANKS][:, 0:w], onehot[:, j, :], ring[:, j, 0:w], start=True,
                              stop=True).then_inc(sums_ready, 1)

        def build_onehot(v, i, j, ahead, table=None):
            v.tensor_scalar(onehot[:, (j + ahead) % U, :], iota[:, :], (dloc if table is None else table)[:, ds(i * U + j + ahead, 1)],
                            None, ALU.is_equal).then_inc(onehot_ready, 1)

        def sum_vector(v, p, m, regs):
            w = widths[p]
            for j in range(HALF):
                build_onehot(v, 0, j, 0)
            with v.Fori(0, TURNS) as i:
                tile = load_tiles(v, regs, i, 0, U)
                for j in range(U):
                    build_onehot(v, i, j, HALF)
                    v.wait_ge(sums_ready, i * U + (U + m * VISITS + j + 1))
                    v.wait_ge(sums_added, i * U + (SUM_BANKS + m * VISITS + j))
                    acc = acc_tile(p, tile[j])
                    v.tensor_tensor(acc, acc, bank[SBANK + j % SUM_BANKS][:, 0:w], ALU.add).then_inc(sums_added, 1)

        def dense_tensor(pe, q, w_in, weights, w_out):
            kb = -(-w_in // P)
            kw = min(w_in, P)
            with pe.Fori(0, TP // 2) as i:
                for u in range(2):
                    pe.wait_ge(d_pre, i * 2 + (q * TP + u + 1))
                    pe.wait_ge(d_evac, i * 2 + (q * TP + 2))
                    if kw == 64:
                        pe.sem_inc(transposes_asked, 1)
                    for k in range(kb):
                        m = pe.transpose(bank[u][0:kw, k * P:(k + 1) * P], pre[:, u, k * kw:(k + 1) * kw], ident[:, 0:P])
                    m.then_inc(d_turned, 1)
                for u in range(2):
                    pe.wait_ge(d_evac, i * 2 + (q * TP + u + 3))
                    pe.wait_ge(d_post, i * 2 + (q * TP + 2))
                    for n, wt in enumerate(weights):
                        for k in range(kb):
                            m = pe.matmul(bank[2 + u + 2 * (n // 2)][:, (n % 2) * w_out:(n % 2 + 1) * w_out],
                                          turned[0:kw, u, k, :], wt(k), start=(k == 0), stop=(k == kb - 1))
                    m.then_inc(d_product, 1)

        def bring(eng, q, src, w, given=None, base=0):
            with eng.Fori(0, TP // 2) as i:
                for u in range(2):
                    eng.wait_ge(d_turned, i * 2 + (q * TP + 2))
                    if given is not None:
                        eng.wait_ge(given, i * 2 + (base + u + 1))
                    eng.tensor_copy(pre[:, u, 0:w], src(i * 2 + u)).then_inc(d_pre, 1)

        def dense_scalar(act, q, w_in, func):
            kb = -(-w_in // P)
            kw = min(w_in, P)
            with act.Fori(0, TP // 2) as i:
                for u in range(2):
                    act.wait_ge(d_turned, i * 2 + (q * TP + u + 3))
                    act.wait_ge(d_product, i * 2 + (q * TP + 2))
                    act.activation(turned[0:kw, u, 0:kb, :], bank[u][0:kw, 0:kb * P].rearrange("p (k n) -> p k n", k=kb),
                                   func).then_inc(d_evac, 1)

        def table_sync(sp, done, base, table, w, off, sem_out):
            with sp.Fori(0, TP // 2) as i:
                sp.wait_ge(done, i * 2 + (base + 2))
                sp.dma_start(table[ds(i * 2 * P, 2 * P), :].rearrange("(t p) d -> p t d", p=P),
                             ACC[:, ds(i * 2 * w + off, 2 * w)].rearrange("p (t d) -> p t d", t=2)).then_inc(sem_out, 16)

        def acc_of(p):
            return lambda t: acc_tile(p, t)

        def x_of(t):
            return X[:, ds(t * D, D)]

        def col(tab, t, w=1):
            return tab[:, ds(t * w, w)]

        def norm_factors(v, st):
            even, odd = moments[:, :, 1], moments[:, :, 4]
            st.link(v.tensor_tensor(mean[:, :], even, odd, ALU.add))
            st.link(v.tensor_scalar(mean[:, :], mean[:, :], 0.5, None, ALU.mult))
            st.link(v.tensor_tensor(root[:, :], even, mean[:, :], ALU.subtract))
            st.link(v.tensor_tensor(root[:, :], root[:, :], root[:, :], ALU.mult))
            st.link(v.tensor_tensor(rstd[:, :], moments[:, :, 2], moments[:, :, 5], ALU.add))
            st.link(v.scalar_tensor_tensor(out=rstd[:, :], in0=rstd[:, :], scalar=1.0 / D, in1=root[:, :],
                                           op0=ALU.mult, op1=ALU.add))
            st.link(v.tensor_scalar(rstd[:, :], rstd[:, :], EPS, None, ALU.add))
            inverse_root(v, st, rstd[:, :], root[:, :], TP)
            st.link(v.scalar_tensor_tensor(out=shift[:, :], in0=mean[:, :], scalar=-1.0, in1=rstd[:, :],
                                           op0=ALU.mult, op1=ALU.mult))

        def after(v, st, q, per, post, pre_=None):
            with v.Fori(0, TP // 2) as i:
                st.enter(i, per)
                if pre_ is not None:
                    for u in range(2):
                        pre_(i * 2 + u, u)
                for u in range(2):
                    v.wait_ge(d_product, i * 2 + (q * TP + u + 3))
                    post(i * 2 + u, u)
                st.leave(TP // 2)

        def scaled_layer_in(v, p, bname):
            w = widths[p]

            def f(t, u):
                v.scalar_tensor_tensor(out=pre[:, u, 0:w], in0=acc_tile(p, t), scalar=col(dis, t), in1=bias[bname][:, :],
                                       op0=ALU.mult, op1=ALU.add).then_inc(d_pre, 1)
            return f

        def product_scaled(v, p):
            def f(t, u):
                v.tensor_scalar(acc_tile(p, t), bank[2 + u][:, 0:widths[p]], col(dis, t), None, ALU.mult).then_inc(d_post, 1)
            return f

        def product_biased(v, st, p, bname):
            w = widths[p]

            def f(t, u):
                st.link(v.scalar_tensor_tensor(out=mid[:, u, 0:w], in0=bank[2 + u][:, 0:w], scalar=col(dis, t),
                                               in1=bias[bname][:, :], op0=ALU.mult, op1=ALU.add))
                v.tensor_scalar(acc_tile(p, t), mid[:, u, 0:w], 0.0, col(dis, t), ALU.max, ALU.mult).then_inc(d_post, 1)
            return f

        def residual_in(v, st, bname, relu):
            def f(t, u):
                st.link(v.scalar_tensor_tensor(out=mid[:, u, :], in0=bank[2 + u][:, 0:D], scalar=col(dis, t),
                                               in1=bias[bname][:, :], op0=ALU.mult, op1=ALU.add))
                if relu:
                    st.link(v.tensor_scalar(mid[:, u, :], mid[:, u, :], 0.0, None, ALU.max))
                st.link(v.tensor_tensor(x_of(t), mid[:, u, :], x_of(t), ALU.add))
                v.bn_stats(col(moments[:, :, :].rearrange("p t s -> p (t s)"), t, 6), x_of(t)).then_inc(d_post, 1)
            return f

        def norm_x(v, st, q):
            v.wait_ge(d_post, q * TP + 2)
            norm_factors(v, st)
            with v.Fori(0, TP // 2) as i:
                for u in range(2):
                    t = i * 2 + u
                    v.tensor_scalar(x_of(t), x_of(t), col(rstd, t), col(shift, t), ALU.mult, ALU.add).then_inc(x_ready, 1)

        def scale_rows(act, p, sem_done):
            with act.Fori(0, TP // 2) as i:
                for u in range(2):
                    t = i * 2 + u
                    act.wait_ge(x_ready, t + 1)
                    act.activation(acc_tile(p, t), x_of(t), ACT.Copy, scale=col(dis, t)).then_inc(sem_done, 1)

        def twice_scaled(v, st, p, bname, sem_done):
            w = widths[p]
            with v.Fori(0, TP // 2) as i:
                st.enter(i, 2)
                for u in range(2):
                    t = i * 2 + u
                    st.link(v.scalar_tensor_tensor(out=mid[:, u, 0:w], in0=acc_tile(p, t), scalar=col(dis, t),
                                                   in1=bias[bname][:, :], op0=ALU.mult, op1=ALU.add))
                    v.tensor_scalar(acc_tile(p, t), mid[:, u, 0:w], col(dis, t), None, ALU.mult).then_inc(sem_done, 1)
                st.leave(TP // 2)

        OH_SUM = VISITS + HALF
        OH_TWO = VISITS + U
        OT_PASS = 2 * (2 * TURNS + 1)
        h3_done = sem("h3_done")
        t7_done = sem("t7_done")

        def turn_onehots(pe, i, h, o, r, hh):
            for q in range(2):
                pe.wait_ge(onehot_ready, i * U + (o + h * HALF + 4 * q + 4))
                pe.wait_ge(ot_copied, i * 4 + (r * OT_PASS + 2 * h + q + 1))
                for c in range(4):
                    t = pe.transpose(bank[q][:, c * P:(c + 1) * P], onehot[:, hh * HALF + 4 * q + c, :], ident[:, 0:P])
                t.then_inc(ot_turned, 1)

        def copy_turned(act, i, h, r, m, hh):
            for q in range(2):
                act.wait_ge(ot_turned, i * 4 + (r * OT_PASS + 2 * h + q + 1))
                act.wait_ge(sums_ready, i * U + (m * VISITS + h * HALF + HALF))
                act.copy(onehotT[:, hh, 4 * q:4 * q + 4, :], bank[q][:, :].rearrange("p (c n) -> p c n", c=4)
                         ).then_inc(ot_copied, 1)

        def score_tensor(pe, o, r, m, regs):
            turn_onehots(pe, 0, 0, o, r, 0)
            with pe.Fori(0, TURNS) as i:
                for h in range(2):
                    turn_onehots(pe, i, h + 1, o, r, 1 - h)
                    tile = load_tiles(pe, regs, i, h * HALF, HALF)
                    for j in range(HALF):
                        if j % 4 == 0:
                            pe.wait_ge(ot_copied, i * 4 + (r * OT_PASS + 2 * h + j // 4 + 3))
                        pe.wait_ge(rows_used, i * U + (h * HALF + j + U - 3))
                        pe.matmul(bank[SBANK + j % SUM_BANKS][:, 0:D], onehotT[:, h, j, :],
                                  ACC[:, ds(tile[j] * D, D)], start=True, stop=True).then_inc(sums_ready, 1)

        def score_scalar(act, r, m):
            copy_turned(act, 0, 0, r, m, 0)
            with act.Fori(0, TURNS) as i:
                for h in range(2):
                    copy_turned(act, i, h + 1, r, m, 1 - h)

        def score_vector(v, g, m):
            for j in range(U):
                build_onehot(v, 0, j, 0)
            with v.Fori(0, TURNS) as i:
                for j in range(U):
                    v.wait_ge(sums_ready, i * U + (U + m * VISITS + j + 1))
                    v.wait_ge(rows_in[j], i * 16 + 16 * (g * TURNS + 1))
                    v.tensor_tensor(message[:, j % 2, :], bank[SBANK + j % SUM_BANKS][:, 0:D], ring[:, j, 0:D],
                                    ALU.mult).then_inc(rows_used, 1)
                    build_onehot(v, i, j, U)
                    v.wait_ge(rows_used, i * U + (U + j + 1))
                    v.tensor_reduce(S[:, ds(i * (U * HEADS) + j * HEADS, HEADS)],
                                    message[:, j % 2, :].rearrange("p (h d) -> p h d", h=HEADS), AX.X,
                                    ALU.add).then_inc(scores_done, 1)

        def running_max(v, st, run_, dst_, tmp_):
            k = 1
            while k < P:
                st.link(v.tensor_tensor(tmp_[:, :, k:P], dst_[:, :, k:P], dst_[:, :, 0:P - k], ALU.is_equal))
                st.link(v.tensor_tensor(tmp_[:, :, k:P], tmp_[:, :, k:P], run_[:, :, 0:P - k], ALU.mult))
                st.link(v.tensor_tensor(run_[:, :, k:P], run_[:, :, k:P], tmp_[:, :, k:P], ALU.max))
                k *= 2

        def blocks(x):
            return x.rearrange("p (b n) -> p b n", n=P)

        GROUP = 4 * P // HEADS
        GROUPS = VISITS // GROUP

        def segment_tensor(pe):
            with pe.Fori(0, GROUPS) as g:
                pe.wait_ge(hs_s, g + 1)
                pe.wait_ge(hs_d, g + 1)
                for b in range(4):
                    pe.transpose(bank[0][:, b * P:(b + 1) * P], st_s[:, b * P:(b + 1) * P], ident[:, 0:P])
                for b in range(4):
                    t = pe.transpose(bank[1][:, b * P:(b + 1) * P], st_d[:, b * P:(b + 1) * P], ident[:, 0:P])
                t.then_inc(hs_turned, 1)
                pe.wait_ge(hs_done, g + 1)
                for b in range(4):
                    t = pe.transpose(bank[2][:, b * P:(b + 1) * P], run[:, b * P:(b + 1) * P], ident[:, 0:P])
                t.then_inc(hs_back, 1)

        def segment_scalar(act):
            act.wait_ge(scores_done, VISITS)
            with act.Fori(0, GROUPS) as g:
                act.copy(st_s, S[:, ds(g * 512, 512)]).then_inc(hs_s, 1)
                act.wait_ge(hs_turned, g + 2)
                act.copy(run, bank[0][:, :]).then_inc(hs_run, 1)
                act.wait_ge(hs_back, g + 1)
                act.copy(ACC[:, ds(g * 512, 512)], bank[2][:, :]).then_inc(hs_out, 1)

        def segment_pool(pool):
            pool.wait_ge(scores_done, VISITS)
            with pool.Fori(0, GROUPS) as g:
                pool.wait_ge(hs_turned, g + 1)
                pool.tensor_copy(st_d.rearrange("p (v h) -> p v h", h=HEADS),
                                 dloc[:, ds(g * GROUP, GROUP)].unsqueeze(2).to_broadcast([P, GROUP, HEADS])
                                 ).then_inc(hs_d, 1)

        def segment_vector(v, st):
            with v.Fori(0, GROUPS) as g:
                st.enter(g, 22)
                v.wait_ge(hs_run, g + 1)
                st.link(v.tensor_copy(run_dst, bank[1][:, :]))
                running_max(v, st, blocks(run), blocks(run_dst), blocks(run_tmp))
                v.tensor_copy(small[:, 30:31], run[:, 0:1]).then_inc(hs_done, 1)
                st.leave(GROUPS)

        def sweep_tensor(pe, o, s, w, src):
            with pe.Fori(0, TURNS) as i:
                for h in range(2):
                    pe.wait_ge(sweep_max, i * U + (s * VISITS + h * HALF + HALF))
                    for j in range(HALF):
                        pe.wait_ge(onehot_ready, i * U + (o + h * HALF + j + 1))
                        t = pe.matmul(bank[h][:, j * w:(j + 1) * w], onehot[:, h * HALF + j, :],
                                      src[:, ds(i * (U * w) + (h * HALF + j) * w, w)], start=True, stop=True)
                    t.then_inc(sweep_ready, 1)

        def sweep_vector(v, s, w, dst, regs):
            part = [dst[:, 0:TP * w]] + [ringf[:, 2560 + k * TP * HEADS:2560 + k * TP * HEADS + TP * w] for k in range(3)]
            for k in range(1, 4):
                v.memset(part[k], 0.0).then_inc(parts_set, 1)
            v.wait_ge(parts_set, 3 * (s + 1))
            for j in range(HALF):
                build_onehot(v, 0, j, 0, dlast)
            with v.Fori(0, TURNS) as i:
                tile = load_tiles(v, regs, i, 0, U)
                for h in range(2):
                    for j in range(HALF):
                        build_onehot(v, i, h * HALF + j, HALF, dlast)
                    v.wait_ge(sweep_ready, i * 2 + (s * 2 * TURNS + h + 1))
                    for j in range(HALF):
                        v.wait_ge(sweep_max, i * U + (U + s * VISITS + h * HALF + j - 3))
                        m = part[j % 4][:, ds(tile[h * HALF + j] * w, w)]
                        v.tensor_tensor(m, m, bank[h][:, j * w:(j + 1) * w], ALU.max).then_inc(sweep_max, 1)

        def join_parts(v, st, s, w, dst):
            v.wait_ge(sweep_max, U + (s + 1) * VISITS)
            for k in range(3):
                st.link(v.tensor_tensor(dst[:, 0:TP * w], dst[:, 0:TP * w],
                                        ringf[:, 2560 + k * TP * HEADS:2560 + k * TP * HEADS + TP * w], ALU.max))

        EXPAND_AT, MINUS_AT = 2, 6

        def expand(pe, i, h, r, b, w, nodes, regs, hh):
            tile = load_tiles(pe, regs, i, h * HALF, HALF)
            pe.wait_ge(ot_copied, i * 4 + (r * OT_PASS + 2 * h + 4))
            pe.wait_ge(weights_minus, i * 2 + (b * (2 * TURNS + 1) + h + 1))
            for j in range(HALF):
                t = pe.matmul(bank[2 + hh][:, j * w:(j + 1) * w], onehotT[:, hh, j, :], nodes[:, ds(tile[j] * w, w)],
                              start=True, stop=True)
            t.then_inc(expand_ready, 1)

        def weighted_tensor(pe, o, r, b, w, nodes, regs, main):
            turn_onehots(pe, 0, 0, o, r, 0)
            expand(pe, 0, 0, r, b, w, nodes, regs, 0)
            with pe.Fori(0, TURNS) as i:
                for h in range(2):
                    turn_onehots(pe, i, h + 1, o, r, 1 - h)
                    for j in range(HALF):
                        if j == EXPAND_AT:
                            expand(pe, i, h + 1, r, b, w, nodes, regs, 1 - h)
                        main(pe, i, h, j)

        def attention_main(pe, i, h, j):
            k = h * HALF + j
            pe.wait_ge(rows_used, i * U + (U + VISITS + k + 1))
            pe.wait_ge(sums_added, i * U + (7 * VISITS + k + 1))
            s = bank[SBANK + j % SUM_BANKS]
            pe.matmul(s[:, 0:AW], onehot[:, k, :], ring[:, k, :], start=True, stop=True).then_inc(sums_ready, 1)

        def gat_main(pe, i, h, j):
            k = h * HALF + j
            pe.wait_ge(rows_in[k], i * 16 + 16 * (9 * TURNS + 1))
            pe.wait_ge(scaled_ready, i * U + (k + 1))
            pe.wait_ge(sums_added, i * U + (8 * VISITS + k + 1))
            s = bank[SBANK + j % SUM_BANKS]
            scaled = message[:, j % 4, 0:P]
            pe.matmul(s[:, 0:GW], scaled, ring[:, k, 0:GW], start=True, stop=True).then_inc(sums_ready, 1)

        def weighted_scalar(act, r, m, b):
            def exps(i, h, hh):
                act.wait_ge(weights_minus, i * 2 + (b * (2 * TURNS + 1) + h + 3))
                if b == 0:
                    to = ring[:, hh * HALF:(hh + 1) * HALF, D:AW]
                    x = minus[:, hh, :].rearrange("p (v h) -> p v h", h=HEADS)
                else:
                    to, x = weight[:, hh, :], minus[:, hh, 0:HALF]
                act.activation(to, x, ACT.Exp).then_inc(weights_ready, 1)
            copy_turned(act, 0, 0, r, m, 0)
            exps(0, 0, 0)
            with act.Fori(0, TURNS) as i:
                for h in range(2):
                    copy_turned(act, i, h + 1, r, m, 1 - h)
                    exps(i, h + 1, 1 - h)

        def attention_minus(v, st, i, h, hh):
            v.wait_ge(expand_ready, i * 2 + (h + 1))
            x = minus[:, hh, :]
            st.link(v.tensor_tensor(x, S[:, ds(i * (U * HEADS) + h * HALF * HEADS, HALF * HEADS)],
                                    bank[2 + hh][:, 0:HALF * HEADS], ALU.subtract))
            v.tensor_scalar(x, x, 0.0, None, ALU.min).then_inc(weights_minus, 1)

        def gat_minus(v, st, i, h, hh):
            v.wait_ge(expand_ready, i * 2 + (2 * TURNS + 1 + h + 1))
            x = minus[:, hh, 0:HALF]
            got = bank[2 + hh][:, 0:2 * HALF].rearrange("p (v k) -> p v k", k=2)
            st.link(v.tensor_tensor(x, asrc[:, ds(i * U + h * HALF, HALF)], got[:, :, 0], ALU.add))
            st.link(v.scalar_tensor_tensor(out=x, in0=x, scalar=0.2, in1=x, op0=ALU.mult, op1=ALU.max))
            st.link(v.tensor_tensor(x, x, got[:, :, 1], ALU.subtract))
            v.tensor_scalar(x, x, 0.0, None, ALU.min).then_inc(weights_minus, 1)

        def weighted_vector(v, st, b, m, aw, minus_, steps, prepare, regs):
            for j in range(U):
                build_onehot(v, 0, j, 0)
            minus_(v, st, 0, 0, 0)
            with v.Fori(0, TURNS) as i:
                st.enter(i, 2 * steps)
                tile = load_tiles(v, regs, i, 0, U)

                def add(k):
                    v.wait_ge(sums_ready, i * U + (U + m * VISITS + k + 1))
                    v.wait_ge(sums_added, i * U + (SUM_BANKS + (7 + b) * VISITS + k))
                    acc = ACC[:, ds(tile[k] * aw, aw)]
                    v.tensor_tensor(acc, acc, bank[SBANK + k % SUM_BANKS][:, 0:aw], ALU.add).then_inc(sums_added, 1)
                    build_onehot(v, i, k, U)

                for h in range(2):
                    v.wait_ge(weights_ready, i * 2 + (b * (2 * TURNS + 1) + h + 1))
                    for j in range(HALF):
                        prepare(v, i, h, j)
                        if j >= 2:
                            add(h * HALF + j - 2)
                        if j == MINUS_AT:
                            minus_(v, st, i, h + 1, 1 - h)
                    add(h * HALF + HALF - 2)
                    add(h * HALF + HALF - 1)
                st.leave(TURNS)

        def weigh_rows(v, i, h, j):
            k = h * HALF + j
            v.wait_ge(rows_in[k], i * 16 + 16 * (8 * TURNS + 1))
            rows = ring[:, k, 0:D].rearrange("p (h d) -> p h d", h=HEADS)
            v.tensor_tensor(rows, rows, ring[:, k, D:AW].unsqueeze(2).to_broadcast([P, HEADS, HD]),
                            ALU.mult).then_inc(rows_used, 1)

        def weigh_onehot(v, i, h, j):
            k = h * HALF + j
            v.tensor_scalar(message[:, j % 4, 0:P], onehot[:, k, :], weight[:, h, j:j + 1], None, ALU.mult
                            ).then_inc(scaled_ready, 1)

        SCALE = float(HD) ** -0.5
        kv_stage = S[:, 0:1024].rearrange("p (k u d) -> p k u d", k=2, u=2)

        def qkv_vector(v, q):
            with v.Fori(0, TP // 2) as i:
                v.wait_ge(kv_out, i * 32 + 32)
                for u in range(2):
                    v.wait_ge(d_product, i * 2 + (q * TP + u + 3))
                    v.tensor_scalar(ACC[:, ds(i * (2 * D) + u * D, D)], bank[2 + u][:, 0:D], SCALE, None,
                                    ALU.mult).then_inc(kv_ready, 1)
                    v.tensor_copy(kv_stage[:, 0, u, :], bank[2 + u][:, D:2 * D]).then_inc(kv_ready, 1)
                    v.tensor_copy(kv_stage[:, 1, u, :], bank[4 + u][:, 0:D]).then_inc(d_post, 1)

        def kv_sync(sp, q):
            sp.sem_inc(kv_out, 32)
            with sp.Fori(0, TP // 2) as i:
                sp.wait_ge(d_post, i * 2 + (q * TP + 4))
                sp.wait_ge(kv_ready, i * 4 + 4)
                for k, table in enumerate((k_table, v_table)):
                    sp.dma_start(table[ds(i * 2 * P, 2 * P), :].rearrange("(t p) d -> p t d", p=P),
                                 kv_stage[:, k]).then_inc(kv_out, 16)

        def y_of(t):
            return ACC[:, ds(t * D, D)]

        moments_f = moments[:, :, :].rearrange("p t s -> p (t s)")

        def attention_out(v, st, q):
            v.wait_ge(weights_ready, 2 * TURNS + 1)
            with v.Fori(0, TP // 2) as i:
                st.enter(i, 6)
                for u in range(2):
                    t = i * 2 + u
                    rec = small[:, 32 + 8 * u:40 + 8 * u]
                    st.link(v.tensor_scalar(rec, ACC[:, ds(t * AW + D, HEADS)], 1e-8, None, ALU.add))
                    st.link(v.reciprocal(rec, rec))
                    v.tensor_tensor(pre[:, u, :].rearrange("p (h d) -> p h d", h=HEADS),
                                    ACC[:, ds(t * AW, D)].rearrange("p (h d) -> p h d", h=HEADS),
                                    rec.unsqueeze(2).to_broadcast([P, HEADS, HD]), ALU.mult).then_inc(d_pre, 1)
                for u in range(2):
                    t = i * 2 + u
                    v.wait_ge(d_product, i * 2 + (q * TP + u + 3))
                    st.link(v.tensor_tensor(mid[:, u, :], bank[2 + u][:, 0:D], bias["L2_gnn_Wo_b"][:, :], ALU.add))
                    v.tensor_tensor(y_of(t), mid[:, u, :], x_of(t), ALU.add).then_inc(y_ready, 1)
                    v.wait_ge(y_ready, t + 1)
                    v.bn_stats(col(moments_f, t, 6), y_of(t)).then_inc(d_post, 1)
                st.leave(TP // 2)

        def norm_gain(v, st, t, u, src, gain, offset):
            st.link(v.tensor_scalar(mid[:, u, :], src, col(rstd, t), col(shift, t), ALU.mult, ALU.add))
            st.link(v.tensor_tensor(mid[:, u, :], mid[:, u, :], gain, ALU.mult))

        def norm_y(v, st, q):
            v.wait_ge(d_post, q * TP + 2)
            norm_factors(v, st)
            with v.Fori(0, TP // 2) as i:
                st.enter(i, 4)
                for u in range(2):
                    t = i * 2 + u
                    norm_gain(v, st, t, u, y_of(t), bias["L2_gnn_ln1_g"][:, :], None)
                    v.tensor_tensor(y_of(t), mid[:, u, :], bias["L2_gnn_ln1_b"][:, :], ALU.add).then_inc(y_ready, 1)
                st.leave(TP // 2)

        def ffn_tensor(pe, q):
            pe.wait_ge(ffn_in, 32)
            with pe.Fori(0, TP // 2) as i:
                for u in range(2):
                    pe.wait_ge(d_pre, i * 2 + (q * TP + u + 1))
                    pe.wait_ge(d_evac, i * 2 + (q * TP + 2))
                    for k in range(2):
                        t = pe.transpose(bank[u][:, k * P:(k + 1) * P], pre[:, u, k * P:(k + 1) * P], ident[:, 0:P])
                    t.then_inc(d_turned, 1)
                for u in range(2):
                    pe.wait_ge(d_evac, i * 2 + (q * TP + u + 3))
                    for f in range(4):
                        for k in range(2):
                            t = pe.matmul(bank[2 + u][:, f * P:(f + 1) * P], fw1[:, k, f * P:(f + 1) * P],
                                          turned[:, u, k, :], start=(k == 0), stop=(k == 1))
                    t.then_inc(h_product, 1)
                for u in range(2):
                    pe.wait_ge(h_done, i * 2 + (u + 1))
                    pe.wait_ge(d_post, i * 2 + (q * TP + 2))
                    for f in range(4):
                        t = pe.matmul(bank[4 + u][:, 0:D], hidden[:, u, f, :], fw2[:, f, :], start=(f == 0), stop=(f == 3))
                    t.then_inc(d_product, 1)

        def ffn_scalar(act, q):
            with act.Fori(0, TP // 2) as i:
                for u in range(2):
                    act.wait_ge(d_turned, i * 2 + (q * TP + u + 3))
                    act.wait_ge(d_product, i * 2 + (q * TP + 2))
                    act.copy(turned[:, u], bank[u][:, 0:D].rearrange("p (k n) -> p k n", k=2)).then_inc(d_evac, 1)
                for u in range(2):
                    act.wait_ge(h_product, i * 2 + (u + 1))
                    for f in range(4):
                        t = act.activation(hidden[:, u, f, :], bank[2 + u][:, f * P:(f + 1) * P], ACT.Gelu,
                                           bias=fb1[:, f:f + 1])
                    t.then_inc(h_done, 1)

        def ffn_vector(v, st, q):
            with v.Fori(0, TP // 2) as i:
                st.enter(i, 4)
                for u in range(2):
                    t = i * 2 + u
                    v.wait_ge(d_product, i * 2 + (q * TP + u + 3))
                    st.link(v.tensor_tensor(mid[:, u, :], bank[4 + u][:, 0:D], bias["L2_gnn_ffn_b2"][:, :], ALU.add))
                    st.link(v.tensor_tensor(y_of(t), mid[:, u, :], y_of(t), ALU.add))
                    v.bn_stats(col(moments_f, t, 6), y_of(t)).then_inc(d_post, 1)
                st.leave(TP // 2)

        def block_residual(v, st, q):
            v.wait_ge(d_post, q * TP + 2)
            norm_factors(v, st)
            with v.Fori(0, TP // 2) as i:
                st.enter(i, 8)
                for u in range(2):
                    t = i * 2 + u
                    norm_gain(v, st, t, u, y_of(t), bias["L2_gnn_ln2_g"][:, :], None)
                    st.link(v.tensor_tensor(mid[:, u, :], mid[:, u, :], bias["L2_gnn_ln2_b"][:, :], ALU.add))
                    st.link(v.tensor_tensor(x_of(t), mid[:, u, :], x_of(t), ALU.add))
                    v.bn_stats(col(moments_f, t, 6), x_of(t)).then_inc(y_ready, 1)
                st.leave(TP // 2)

        def xp_vector(v, q):
            with v.Fori(0, TP // 2) as i:
                for u in range(2):
                    t = i * 2 + u
                    v.wait_ge(d_product, i * 2 + (q * TP + u + 3))
                    v.tensor_copy(ACC[:, ds(t * GW, D)], bank[2 + u][:, 0:D])
                    v.tensor_copy(node_src[:, ds(t, 1)], bank[2 + u][:, D:D + 1])
                    v.tensor_copy(node_e[:, :, :].rearrange("p t k -> p (t k)")[:, ds(t * 2, 1)],
                                  bank[2 + u][:, D + 1:D + 2]).then_inc(d_post, 1)

        def xp_sync(sp, q):
            with sp.Fori(0, TP // 2) as i:
                sp.wait_ge(d_post, i * 2 + (q * TP + 4))
                sp.dma_start(xp_table[ds(i * 2 * P, 2 * P), :].rearrange("(t p) d -> p t d", p=P),
                             ACC[:, ds(i * 2 * GW, 2 * GW)].rearrange("p (t d) -> p t d", t=2)[:, :, 0:D]).then_inc(xp_out, 16)

        GQ = U // 4

        def sources_sync(sp):
            sp.sem_inc(tile_onehot_built, 2)
            with sp.Fori(0, TURNS // 2) as i:
                for b in range(2):
                    sp.wait_ge(tile_onehot_built, i * 2 + (b + 1))
                    sp.dma_start(src_hi[:, b, :], hi_rows[ds(i * 2 * U + b * U, U), :].rearrange("(o v) e -> o (v e)", o=1)
                                 .to_broadcast([TP, U * P])).then_inc(hi_in[b], 16)

        def sources_pool(pool):
            pool.sem_inc(row_looked_up, 2 * GQ)
            pool.wait_ge(src_rows_ready, 1)
            with pool.Fori(0, TURNS // 2) as i:
                for b in range(2):
                    pool.wait_ge(hi_in[b], i * 16 + 16)
                    pool.wait_ge(row_looked_up, i * (2 * GQ) + (b * GQ + GQ))
                    pool.sem_inc(tile_onehots_asked, 1)
                    pool.tensor_scalar(tile_onehot[:, b, :], src_hi[:, b, :], small[0:TP, 17:18], None, ALU.is_equal
                                       ).then_inc(tile_onehot_built, 1)

        def sources_tensor(pe):
            pe.sem_inc(src_taken, U)
            pe.wait_ge(src_rows_ready, 1)
            with pe.Fori(0, TURNS // 2) as i:
                for b in range(2):
                    pe.wait_ge(tile_onehot_built, i * 2 + (b + 3))
                    for q in range(GQ):
                        pe.wait_ge(src_taken, i * (2 * U) + (b * U + 4 * q + 4))
                        for c in range(4):
                            e = (4 * q + c) * P
                            t = pe.matmul(bank[SBANK + q][:, c * P:(c + 1) * P], tile_onehot[:, b, e:e + P],
                                          src_rows, start=True, stop=True)
                        t.then_inc(row_looked_up, 1)

        def sources_vector(v):
            with v.Fori(0, TURNS // 2) as i:
                for b in range(2):
                    for q in range(GQ):
                        v.wait_ge(row_looked_up, i * (2 * GQ) + (b * GQ + q + 1 + 2 * GQ))
                        v.wait_ge(src_taken, i * (2 * U) + (b * U + 4 * q + 4))
                        if q % 2 == 0:
                            v.wait_ge(src_copied, i * 4 + (2 * b + q // 2 + 1))
                        for c in range(4):
                            j = 4 * q + c
                            v.scalar_tensor_tensor(out=onehot[:, j, :], in0=iota[:, :],
                                                   scalar=src_lo[:, ds(i * (2 * U) + b * U + j, 1)],
                                                   in1=bank[SBANK + q][:, c * P:(c + 1) * P], op0=ALU.is_equal,
                                                   op1=ALU.mult, accum_out=src_now[:, j:j + 1]).then_inc(src_taken, 1)

        def sources_scalar(act):
            with act.Fori(0, TURNS) as i:
                for h in range(2):
                    act.wait_ge(src_taken, i * U + (U + HALF * (h + 1)))
                    act.copy(asrc[:, ds(i * U + h * HALF, HALF)], src_now[:, h * HALF:(h + 1) * HALF]).then_inc(src_copied, 1)

        def least_tensor(pe):
            pe.wait_ge(src_up, 1)
            pe.transpose(bank[0][0:TP, 0:P], node_src[:, :], ident[:, 0:P]).then_inc(src_turned, 1)
            pe.wait_ge(least_step, 1)
            pe.transpose(bank[2][0:1, 0:P], small[:, 50:51], ident[:, 0:P]).then_inc(least_turned, 1)
            pe.wait_ge(least_step, 2)
            pe.matmul(bank[3][:, 0:1], ones[0:1, :], small[0:1, 51:52], start=True, stop=True).then_inc(least_turned, 1)

        L3_GROUPS = [(0, 4), (4, VB - 4)]

        def gat_segment_tensor(pe):
            for g, (b0, nb) in enumerate(L3_GROUPS):
                pe.wait_ge(src_up, 2)
                if g:
                    pe.wait_ge(hs_out, GROUPS + g)
                for b in range(nb):
                    pe.transpose(bank[0][:, b * P:(b + 1) * P], asrc_up[:, (b0 + b) * P:(b0 + b + 1) * P], ident[:, 0:P])
                for b in range(nb):
                    t = pe.transpose(bank[1][:, b * P:(b + 1) * P], dloc[:, (b0 + b) * P:(b0 + b + 1) * P], ident[:, 0:P])
                t.then_inc(hs_turned, 1)
                pe.wait_ge(hs_done, GROUPS + g + 1)
                for b in range(nb):
                    t = pe.transpose(bank[2][:, b * P:(b + 1) * P], run[:, b * P:(b + 1) * P], ident[:, 0:P])
                t.then_inc(hs_back, 1)

        def gat_segment_scalar(act):
            for g, (b0, nb) in enumerate(L3_GROUPS):
                act.wait_ge(hs_turned, GROUPS + g + 2)
                act.copy(run[:, 0:nb * P], bank[0][:, 0:nb * P]).then_inc(hs_run, 1)
                act.wait_ge(hs_back, GROUPS + g + 1)
                act.copy(run_src[:, b0 * P:(b0 + nb) * P], bank[2][:, 0:nb * P]).then_inc(hs_out, 1)

        def gat_segment_vector(v, st):
            for g, (b0, nb) in enumerate(L3_GROUPS):
                v.wait_ge(hs_run, GROUPS + g + 1)
                st.link(v.tensor_copy(run_dst[:, 0:nb * P], bank[1][:, 0:nb * P]))
                running_max(v, st, blocks(run[:, 0:nb * P]), blocks(run_dst[:, 0:nb * P]), blocks(run_tmp[:, 0:nb * P]))
                v.tensor_copy(small[:, 30:31], run[:, 0:1]).then_inc(hs_done, 1)

        def gat_maxima_before(v, st, q):
            v.wait_ge(d_post, q * TP + 2)
            v.sem_inc(src_up, 1)
            v.wait_ge(src_turned, 1)
            v.tensor_copy(src_rows, bank[0][0:TP, 0:P]).then_inc(src_rows_ready, 1)
            v.tensor_reduce(small[:, 50:51], node_src[:, :], AX.X, ALU.min).then_inc(least_step, 1)
            v.wait_ge(least_turned, 1)
            v.tensor_reduce(small[0:1, 51:52], bank[2][0:1, 0:P], AX.X, ALU.min).then_inc(least_step, 1)
            v.wait_ge(least_turned, 2)
            st.link(v.tensor_copy(small[:, 52:53], bank[3][:, 0:1]))
            st.link(v.tensor_scalar(node_max[:, 0:TP], node_src[:, :], small[:, 52:53], None, ALU.subtract))
            st.link(v.memset(asrc[:, VISITS:VT], 0.0))
            st.link(v.tensor_scalar(asrc_up.bitcast(I32), idx_tab[:, :], P - 1, None, ALU.bitwise_and))
            st.link(v.tensor_copy(src_lo, asrc_up.bitcast(I32)))
            sources_vector(v)
            v.wait_ge(src_copied, 2 * TURNS + 2)
            v.tensor_scalar(asrc_up, asrc, small[:, 52:53], None, ALU.subtract).then_inc(src_up, 1)

        def gat_maxima_after(v, st):
            e_max, a_dst = node_e[:, :, 1], node_e[:, :, 0]
            st.link(v.tensor_scalar(node_max[:, 0:TP], node_max[:, 0:TP], small[:, 52:53], None, ALU.add))
            st.link(v.tensor_tensor(node_max[:, 0:TP], node_max[:, 0:TP], node_src[:, :], ALU.max))
            st.link(v.tensor_tensor(node_max[:, 0:TP], node_max[:, 0:TP], a_dst, ALU.add))
            st.link(v.scalar_tensor_tensor(out=e_max, in0=node_max[:, 0:TP], scalar=0.2, in1=node_max[:, 0:TP],
                                           op0=ALU.mult, op1=ALU.max))
            st.link(v.tensor_tensor(node_self, node_src[:, :], a_dst, ALU.add))
            st.link(v.scalar_tensor_tensor(out=node_self, in0=node_self, scalar=0.2, in1=node_self,
                                           op0=ALU.mult, op1=ALU.max))
            st.link(v.tensor_tensor(node_self, node_self, e_max, ALU.subtract))
            v.tensor_scalar(node_self, node_self, 0.0, None, ALU.min).then_inc(self_ready, 1)
            v.wait_ge(self_ready, 2)
            v.wait_ge(xp_out, 16 * (TP // 2))
            with v.Fori(0, TP) as t:
                v.tensor_scalar(ACC[:, ds(t * GW, D)], ACC[:, ds(t * GW, D)], node_self[:, ds(t, 1)], None, ALU.mult)
                v.tensor_copy(ACC[:, ds(t * GW + D, 1)], node_self[:, ds(t, 1)]).then_inc(acc_zero, 1)

        def gru_vector(v, st, q):
            with v.Fori(0, TP // 2) as i:
                st.enter(i, 6)
                for u in range(2):
                    t = i * 2 + u
                    rec = small[:, 32 + u:33 + u]
                    st.link(v.reciprocal(rec, ACC[:, ds(t * GW + D, 1)]))
                    v.scalar_tensor_tensor(out=pre[:, u, :], in0=ACC[:, ds(t * GW, D)], scalar=rec,
                                           in1=bias["L3_gnn_bias"][:, :], op0=ALU.mult, op1=ALU.add).then_inc(d_pre, 1)
                for u in range(2):
                    v.wait_ge(gates_ready, i * 2 + (u + 1))
                    v.tensor_tensor(mid[:, u, :], gates[:, u, 0, :], gates[:, u, 1, :], ALU.mult).then_inc(cell_ready, 1)
                for u in range(2):
                    t = i * 2 + u
                    v.wait_ge(cell_tanh, i * 2 + (u + 1))
                    st.link(v.tensor_tensor(mid[:, u, :], gates[:, u, 2, :], gates[:, u, 0, :], ALU.mult))
                    st.link(v.tensor_tensor(x_of(t), mid[:, u, :], x_of(t), ALU.add))
                    v.bn_stats(col(moments_f, t, 6), x_of(t)).then_inc(d_post, 1)
                st.leave(TP // 2)

        def gru_scalar(act, q):
            with act.Fori(0, TP // 2) as i:
                for u in range(2):
                    act.wait_ge(d_turned, i * 2 + (q * TP + u + 3))
                    act.wait_ge(d_product, i * 2 + (q * TP + 2))
                    act.activation(turned[:, u], bank[u][:, 0:D].rearrange("p (k n) -> p k n", k=2),
                                   ACT.Tanh).then_inc(d_evac, 1)
                for u in range(2):
                    act.wait_ge(d_product, i * 2 + (q * TP + u + 3))
                    act.wait_ge(d_post, i * 2 + (q * TP + 2))
                    act.activation(gates[:, u, 0, :], bank[2 + u][:, 0:D], ACT.Sigmoid)
                    act.activation(gates[:, u, 1, :], bank[2 + u][:, D:2 * D], ACT.Tanh)
                    act.activation(gates[:, u, 2, :], bank[4 + u][:, 0:D], ACT.Sigmoid).then_inc(gates_ready, 1)
                for u in range(2):
                    act.wait_ge(cell_ready, i * 2 + (u + 1))
                    act.activation(gates[:, u, 0, :], mid[:, u, :], ACT.Tanh).then_inc(cell_tanh, 1)

        @block.sync
        def _(sp):
            setup_sync(sp)
            dbase = {0: (d_post, 2), 1: (d_post, TP + 2), 2: (d_post, 2 * TP + 2), 3: (h3_done, 0), 4: (d_post, 3 * TP + 2),
                     5: (d_post, 4 * TP + 2), 6: (t7_done, 0)}
            for p in range(7):
                done, base = dbase[p]
                table_sync(sp, done, base, tables[p], widths[p], accoff[p], table_out)
            for n, name in enumerate(("L2_gnn_Wq", "L2_gnn_Wk", "L2_gnn_Wv")):
                sp.dma_start(Wqkv[:, n], a[name].rearrange("(k p) n -> p k n", p=P)).then_inc(qkv_in, 16)
            kv_sync(sp, 7)
            sp.wait_ge(sums_added, SUM_BANKS + 8 * VISITS)
            sp.dma_start(fw1, a["L2_gnn_ffn_w1"].rearrange("(k p) n -> p k n", p=P)).then_inc(ffn_in, 16)
            sp.dma_start(fw2, a["L2_gnn_ffn_w2"].rearrange("(k p) n -> p k n", p=P)).then_inc(ffn_in, 16)
            xp_sync(sp, 10)
            sources_sync(sp)
            sp.wait_ge(x_ready, 4 * TP)
            sp.dma_start(out[0:(N // P) * P, :].rearrange("(t p) d -> p t d", p=P),
                         X[:, 0:(N // P) * D].rearrange("p (t d) -> p t d", d=D)).then_inc(out_done, 16)
            sp.dma_start(out[(N // P) * P:N, :], X[0:N % P, (TILES - 1) * D:TILES * D]).then_inc(out_done, 16)
            sp.wait_ge(out_done, 32)

        @block.gpsimd
        def _(pool):
            setup_pool(pool)
            pool.wait_ge(x_in, 32)
            bring(pool, 0, x_of, D)
            for p in range(7):
                gather_rows(pool, p, tables[p], widths[p], sums_ready, p * VISITS, 16 * (TP // 2) * (p + 1))
                if p >= 3:
                    pool.wait_ge(sums_added, SUM_BANKS + (p + 1) * VISITS)
                    bring(pool, p, acc_of(p), widths[p])

            bring(pool, 7, x_of, D, x_ready, TP)
            stored = 32 + 32 * (TP // 2)
            gather_rows(pool, 7, k_table, D, rows_used, 0, stored, kv_out)
            segment_pool(pool)
            pool.wait_ge(hs_out, GROUPS)
            pool.wait_ge(parts_joined, 1)
            gather_rows(pool, 8, v_table, D, sums_ready, 8 * VISITS, stored, kv_out)
            bring(pool, 9, y_of, D, y_ready, TP)
            bring(pool, 10, x_of, D, x_ready, 2 * TP)
            sources_pool(pool)
            pool.wait_ge(hs_out, GROUPS + len(L3_GROUPS))
            pool.wait_ge(parts_joined, 2)
            gather_rows(pool, 9, xp_table, D, sums_ready, 9 * VISITS, 16 * (TP // 2), xp_out)

        @block.tensor
        def _(pe):
            setup_tensor(pe)
            pe.wait_ge(weights_in, 16 * 8)
            pe.wait_ge(x_in, 32)
            pe.wait_ge(weight_copied, len(nat_blocks) + 1)
            dense_tensor(pe, 0, D, [lambda k: W1[:, k, :]], 128)
            sum_tensor(pe, 0, 0, 0, 0)
            dense_tensor(pe, 1, 128, [lambda k: W2[:, :]], 64)
            sum_tensor(pe, 1, 1, 1, OH_SUM)
            dense_tensor(pe, 2, 64, [lambda k: W3[:, :]], 32)
            sum_tensor(pe, 2, 2, 2, 2 * OH_SUM)
            sum_tensor(pe, 3, 3, 3, 3 * OH_SUM)
            dense_tensor(pe, 3, 32, [lambda k: W4[:, :]], 64)
            sum_tensor(pe, 4, 4, 4, 4 * OH_SUM)
            dense_tensor(pe, 4, 64, [lambda k: W5[:, :]], 128)
            sum_tensor(pe, 5, 5, 5, 5 * OH_SUM)
            dense_tensor(pe, 5, 128, [lambda k: W6[:, :]], 256)
            sum_tensor(pe, 6, 6, 6, 6 * OH_SUM)
            dense_tensor(pe, 6, 256, [lambda k: L1T[:, k, :]], 256)
            pe.wait_ge(qkv_in, 48)
            dense_tensor(pe, 7, 256, [lambda k, n=n: Wqkv[:, n, k, :] for n in range(3)], 256)
            regs = [pe.alloc_register(f"pe_tile{j}") for j in range(HALF)]
            o = 7 * OH_SUM
            score_tensor(pe, o, 0, 7, regs)
            o += OH_TWO
            segment_tensor(pe)
            pe.wait_ge(hs_out, GROUPS)
            sweep_tensor(pe, o, 0, HEADS, ACC)
            o += OH_SUM
            pe.wait_ge(acc_zero, 1)
            weighted_tensor(pe, o, 1, 0, HEADS, node_max, regs, attention_main)
            o += OH_TWO
            dense_tensor(pe, 8, 256, [lambda k: Wo[:, k, :]], 256)
            ffn_tensor(pe, 9)
            dense_tensor(pe, 10, 256, [lambda k: L3T[:, k, :]], 258)
            least_tensor(pe)
            sources_tensor(pe)
            gat_segment_tensor(pe)
            pe.wait_ge(hs_out, GROUPS + len(L3_GROUPS))
            sweep_tensor(pe, o, 1, 1, run_src)
            o += OH_SUM
            pe.wait_ge(acc_zero, 1 + TP)
            weighted_tensor(pe, o, 2, 1, 2, node_e[:, :, :].rearrange("p t k -> p (t k)"), regs, gat_main)
            dense_tensor(pe, 11, 256, [lambda k, n=n: WihT[:, k, n * D:(n + 1) * D] for n in range(3)], 256)

        @block.scalar
        def _(act):
            setup_scalar(act)
            take_root(act, dis[:, 0:TILES], root[:, 0:TILES])
            dense_scalar(act, 0, D, ACT.Copy)
            dense_scalar(act, 1, 128, ACT.Relu)
            dense_scalar(act, 2, 64, ACT.Relu)
            dense_scalar(act, 3, 32, ACT.Copy)
            dense_scalar(act, 4, 64, ACT.Copy)
            dense_scalar(act, 5, 128, ACT.Copy)
            take_root(act, rstd[:, :], root[:, :])
            scale_rows(act, 6, t7_done)
            dense_scalar(act, 6, 256, ACT.Copy)
            take_root(act, rstd[:, :], root[:, :])
            dense_scalar(act, 7, 256, ACT.Copy)
            score_scalar(act, 0, 7)
            segment_scalar(act)
            weighted_scalar(act, 1, 8, 0)
            dense_scalar(act, 8, 256, ACT.Copy)
            take_root(act, rstd[:, :], root[:, :])
            ffn_scalar(act, 9)
            take_root(act, rstd[:, :], root[:, :])
            take_root(act, rstd[:, :], root[:, :])
            dense_scalar(act, 10, 256, ACT.Copy)
            sources_scalar(act)
            gat_segment_scalar(act)
            act.wait_ge(self_ready, 1)
            act.activation(node_self, node_self, ACT.Exp).then_inc(self_ready, 1)
            weighted_scalar(act, 2, 9, 1)
            gru_scalar(act, 11)
            take_root(act, rstd[:, :], root[:, :])

        @block.vector
        def _(v):
            st = Steps(v, vec)
            regs = [v.alloc_register(f"tile_reg{j}") for j in range(U)]
            setup_vector(v, st)
            v.wait_ge(bias_in, 16 * len(BIAS_W))
            after(v, st, 0, 0, product_scaled(v, 0))
            sum_vector(v, 0, 0, regs)
            after(v, st, 1, 0, product_scaled(v, 1), scaled_layer_in(v, 0, "L0_gnn_b1"))
            sum_vector(v, 1, 1, regs)
            after(v, st, 2, 0, product_scaled(v, 2), scaled_layer_in(v, 1, "L0_gnn_b2"))
            sum_vector(v, 2, 2, regs)
            twice_scaled(v, st, 2, "L0_gnn_b3", h3_done)
            sum_vector(v, 3, 3, regs)
            after(v, st, 3, 2, product_biased(v, st, 4, "L0_gnn_b4"))
            sum_vector(v, 4, 4, regs)
            after(v, st, 4, 2, product_biased(v, st, 5, "L0_gnn_b5"))
            sum_vector(v, 5, 5, regs)
            after(v, st, 5, 4, residual_in(v, st, "L0_gnn_b6", False))
            norm_x(v, st, 6)
            sum_vector(v, 6, 6, regs)
            after(v, st, 6, 6, residual_in(v, st, "L1_gnn_b", True))
            norm_x(v, st, 7)
            qkv_vector(v, 7)
            v.wait_ge(kv_out, 32 + 32 * (TP // 2))
            v.memset(node_max[:, :], 0.0)
            score_vector(v, 7, 7)
            segment_vector(v, st)
            v.wait_ge(hs_out, GROUPS)
            sweep_vector(v, 0, HEADS, node_max, regs)
            join_parts(v, st, 0, HEADS, node_max)
            v.sem_inc(parts_joined, 1)
            v.memset(ACC[:, :], 0.0).then_inc(acc_zero, 1)
            weighted_vector(v, st, 0, 8, AW, attention_minus, 1, weigh_rows, regs)
            attention_out(v, st, 8)
            norm_y(v, st, 9)
            ffn_vector(v, st, 9)
            block_residual(v, st, 10)
            v.wait_ge(y_ready, 3 * TP)
            norm_x(v, st, 10)
            xp_vector(v, 10)
            gat_maxima_before(v, st, 11)
            gat_segment_vector(v, st)
            v.wait_ge(hs_out, GROUPS + len(L3_GROUPS))
            sweep_vector(v, 1, 1, node_max, regs)
            join_parts(v, st, 1, 1, node_max)
            v.memset(ring[:, :, D:GW], 1.0).then_inc(parts_joined, 1)
            gat_maxima_after(v, st)
            weighted_vector(v, st, 1, 9, GW, gat_minus, 3, weigh_onehot, regs)
            gru_vector(v, st, 11)
            norm_x(v, st, 12)


_INS = ['x', 'src', 'dst', 'L0_gnn_W1', 'L0_gnn_b1', 'L0_gnn_W2', 'L0_gnn_b2', 'L0_gnn_W3', 'L0_gnn_b3',
        'L0_gnn_W4', 'L0_gnn_b4', 'L0_gnn_W5', 'L0_gnn_b5', 'L0_gnn_W6', 'L0_gnn_b6', 'L1_gnn_W', 'L1_gnn_b',
        'L2_gnn_Wq', 'L2_gnn_Wk', 'L2_gnn_Wv', 'L2_gnn_Wo_w', 'L2_gnn_Wo_b', 'L2_gnn_ln1_g', 'L2_gnn_ln1_b',
        'L2_gnn_ln2_g', 'L2_gnn_ln2_b', 'L2_gnn_ffn_w1', 'L2_gnn_ffn_b1', 'L2_gnn_ffn_w2', 'L2_gnn_ffn_b2',
        'L3_gnn_W', 'L3_gnn_att_src', 'L3_gnn_att_dst', 'L3_gnn_bias', 'L3_gnn_W_ih', 'L3_gnn_W_hh']


def kernel(**inputs):
    import numpy as _np
    import concourse.bacc as _bacc
    from concourse import mybir as _mybir
    from concourse.bass_utils import run_bass_kernel_spmd as _run

    nc = _bacc.Bacc("TRN2", target_bir_lowering=False, num_devices=1)
    arrays, args = {}, {}
    for name in _INS:
        x = _np.ascontiguousarray(inputs[name])
        arrays[f"in_{name}_dram"] = x
        args[name] = nc.dram_tensor(f"in_{name}_dram", x.shape, _mybir.dt.from_np(x.dtype), kind="ExternalInput").ap()
    out = nc.dram_tensor("out_0_dram", (N, D), F32, kind="ExternalOutput").ap()
    build_program(nc, args, out)
    r = _run(nc, [arrays], core_ids=[0])
    return r.results[0]["out_0_dram"]
```

```python
from contextlib import ExitStack

import concourse.bass as bass
from concourse import mybir

F32 = mybir.dt.float32
I32 = mybir.dt.int32
BF16 = mybir.dt.bfloat16
ALU = mybir.AluOpType
ACT = mybir.ActivationFunctionType
AX = mybir.AxisListType
DVE = mybir.EngineType.DVE
PE = mybir.EngineType.PE
ds = bass.ds

P = 128
N = 6250
E = 100000
D = 256
TILES = -(-N // P)
TP = TILES + TILES % 2
NP = TP * P
CHUNKS = -(-E // P)
U = 16
HALF = U // 2
TURNS = -(-(CHUNKS + TILES - 1) // U)
VISITS = TURNS * U
VT = -(-(VISITS + U) // P) * P
VB = VT // P
CROWS = CHUNKS + 2
NO_NODE = 1 << 20
HEADS = 8
HD = D // HEADS
EC, EP = 800, 125
SUM_BANKS = 4
SBANK = 4
BIAS_W = {"L0_gnn_b1": 128, "L0_gnn_b2": 64, "L0_gnn_b3": 32, "L0_gnn_b4": 64, "L0_gnn_b5": 128,
          "L0_gnn_b6": 256, "L1_gnn_b": 256, "L2_gnn_Wo_b": 256, "L2_gnn_ln1_g": 256, "L2_gnn_ln1_b": 256,
          "L2_gnn_ln2_g": 256, "L2_gnn_ln2_b": 256, "L2_gnn_ffn_b2": 256, "L3_gnn_bias": 256}
EPS = 1e-5


class Steps:

    def __init__(self, eng, sem):
        self.eng, self.sem, self.base, self.n, self.i, self.per = eng, sem, 0, 0, None, 0

    def link(self, ins):
        ins.then_inc(self.sem, 1)
        self.n += 1
        self.eng.wait_ge(self.sem, self.base + self.n if self.i is None else self.i * self.per + (self.base + self.n))

    def mark(self, ins):
        ins.then_inc(self.sem, 1)
        self.n += 1
        return self.n

    def reached(self, n):
        self.eng.wait_ge(self.sem, self.base + n if self.i is None else self.i * self.per + (self.base + n))

    def enter(self, i, per):
        self.base += self.n
        self.i, self.per, self.n = i, per, 0

    def leave(self, turns):
        assert self.n == self.per, (self.n, self.per)
        self.base += self.per * turns
        self.n, self.i = 0, None


def build_program(nc, a, out, last_stage=99):
    ctx = ExitStack()
    with ctx:
        def sb(name, shape, dt=F32):
            return ctx.enter_context(nc.sbuf_tensor(name, shape, dt))

        def sem(name):
            return ctx.enter_context(nc.semaphore(name))

        X = sb("X", [P, TP * D])
        ACC = sb("ACC", [P, TP * (D + HEADS)])
        S = sb("S", [P, (VISITS + HALF) * HEADS])
        ring = sb("ring", [P, U, D + HEADS])
        idx_tab = sb("idx_tab", [P, VT], I32)
        idx_now = sb("idx_now", [P, U], I32)
        dloc = sb("dloc", [P, VT])
        dlast = sb("dlast", [P, VT])
        tile_of = sb("tile_of", [1, VT], I32)
        dis = sb("dis", [P, TP])
        onehot = sb("onehot", [P, U, P])
        iota = sb("iota", [P, P])
        ident = sb("ident", [P, P + 1])
        ones = sb("ones", [P, P])
        onehotT = sb("onehotT", [P, 2, HALF, P])
        message = sb("message", [P, 4, D])
        early = message[:, :, :].rearrange("p u d -> p (u d)")
        W1 = early[:, 0:256].rearrange("p (k n) -> p k n", k=2)
        W6 = early[:, 256:512]
        early_bias = {"L0_gnn_b1": early[:, 512:640], "L0_gnn_b5": early[:, 640:768], "L0_gnn_b6": early[:, 768:1024]}
        bias = {n: early_bias[n] if n in early_bias else sb("bc_" + n, [P, w]) for n, w in BIAS_W.items()}
        Wqkv = S[:, 1100:1100 + 6 * D].rearrange("p (w k n) -> p w k n", w=3, k=2)
        weight = sb("weight", [P, 2, HALF])
        minus = sb("minus", [P, 2, HALF * HEADS])
        node_max = sb("node_max", [P, TP * HEADS])
        node_src = sb("node_src", [P, TP])
        node_e = sb("node_e", [P, TP, 2])
        src_now = sb("src_now", [P, U])
        small = sb("small", [P, 64])
        moments = sb("moments", [P, TP, 6])
        mean = sb("mean", [P, TP])
        rstd = sb("rstd", [P, TP])
        tmp2 = sb("tmp2", [P, TP])
        shift = sb("shift", [P, TP])
        root = sb("root", [P, TP])
        W2 = sb("W2", [128, 64])
        W3 = sb("W3", [64, 32])
        W4 = sb("W4", [32, 64])
        W5 = sb("W5", [64, 128])
        L1T = sb("L1T", [P, 2, D])
        L3T = sb("L3T", [P, 2, D + 2])
        WihT = sb("WihT", [P, 2, 3 * D])
        Wo = sb("Wo", [P, 2, D])
        fb1 = sb("fb1", [P, 4])

        def accv(lo, n, dt=F32, p=P):
            v = ACC[0:p, lo:lo + n]
            return v if dt == F32 else v.bitcast(dt)

        dst_i = accv(0, EC, I32, EP)
        hi_i = accv(800, EC, I32, EP)
        lo_i = accv(1600, EC, I32, EP)
        hi_f = accv(2400, EC, F32, EP)
        lo_f = accv(3200, EC, F32, EP)
        edge_i = accv(4000, VB * 2 * P, I32).rearrange("p (k w) -> p k w", k=VB)
        edge_f = accv(5800, VB * 2 * P).rearrange("p (k w) -> p k w", k=VB)
        passed = accv(7600, VT, F32, TILES - 1)
        viota = accv(8500, VT)
        tri = accv(9400, P)
        hist = accv(9530, P, F32, TILES)
        dnext = accv(9700, VT)
        viota_i = accv(10600, VT, I32)
        hi_i_rows = accv(11500, VT, I32).rearrange("p (k e) -> p k e", k=VB)
        hi_b_rows = accv(12400, VT // 2).bitcast(BF16).rearrange("p (k e) -> p k e", k=VB)
        nat_L1 = S[:, 0:512].rearrange("p (o d) -> p o d", o=2)
        nat_L3 = S[:, 512:1024].rearrange("p (o d) -> p o d", o=2)
        nat_ih = S[:, 1024:2560].rearrange("p (o d) -> p o d", o=6)
        att = S[:, 2560:2564]
        oh_lo = S[0:EP, 2600:2600 + 2048].bitcast(BF16).rearrange("p (b c n) -> p b c n", b=2, c=U)
        oh_hi = S[0:EP, 4700:4700 + U * TILES].bitcast(BF16).rearrange("p (b c n) -> p b c n", b=2, c=U)
        fw1 = S[:, 0:1024].rearrange("p (k n) -> p k n", k=2)
        fw2 = S[:, 1024:2048].rearrange("p (k n) -> p k n", k=4)
        asrc = S[:, 2048:2048 + VT]
        asrc_up = S[:, 3072:3072 + VT]
        run_src = S[:, 4096:4096 + VT]
        node_self = S[:, 5000:5000 + TP]
        src_rows = S[0:TP, 5100:5100 + P]
        src_hi = S[0:TP, 0:U * P].bitcast(BF16).rearrange("p (b e) -> p b e", b=2)
        src_lo = S[:, 5240:5240 + VT]
        iota_b = S[:, 5600:5664].bitcast(BF16)
        zero_b = S[:, 5700:5764].bitcast(BF16)
        pad_i = S[0:2, 5800:5800 + 2 * P].bitcast(I32)

        ringf = ring[:, :, :].rearrange("p u d -> p (u d)")
        turned = ringf[:, 0:512].rearrange("p (b k n) -> p b k n", b=2, k=2)
        pre = ringf[:, 1024:1536].rearrange("p (b n) -> p b n", b=2)
        hidden = ringf[:, 2048:3072].rearrange("p (b f n) -> p b f n", b=2, f=4)
        gates = ringf[:, 2048:3584].rearrange("p (b g n) -> p b g n", b=2, g=3)
        tile_onehot = ringf[0:TP, 0:2 * U * P].rearrange("p (b e) -> p b e", b=2)
        st_s = ringf[:, 0:512]
        st_d = ringf[:, 512:1024]
        run = ringf[:, 1024:1536]
        run_tmp = ringf[:, 1536:2048]
        run_dst = ringf[:, 2048:2560]
        mid = ringf[:, 1536:2048].rearrange("p (b n) -> p b n", b=2)

        bank = [ctx.enter_context(nc.psum_tensor(f"bank{i}", [P, 512], F32)) for i in range(8)]

        edges_d = nc.dram_tensor("edges_d", (CROWS, 2 * P), I32).ap()
        widths = [128, 64, 32, 32, 64, 128, 256]
        tables = [nc.dram_tensor(f"table{p}", (NP, w), F32).ap() for p, w in enumerate(widths)]
        k_table = nc.dram_tensor("k_table", (NP, D), F32).ap()
        v_table = nc.dram_tensor("v_table", (NP, D), F32).ap()
        xp_table = nc.dram_tensor("xp_table", (NP, D), F32).ap()
        hi_rows = nc.dram_tensor("hi_rows", (VT, P), BF16).ap()
        AW = D + HEADS
        GW = D + 1
        accoff = [0, 0, 0, 0, 1600, 4800, 0]

        def acc_tile(p, t):
            return ACC[:, ds(t * widths[p] + accoff[p], widths[p])]

        x_in = sem("x_in")
        pads_set = sem("pads_set")
        edges_in = sem("edges_in")
        edges_padded = sem("edges_padded")
        dst_in = sem("dst_in")
        weights_in = sem("weights_in")
        natural_in = sem("natural_in")
        bias_in = sem("bias_in")
        consts_set = sem("consts_set")
        x_tail_set = sem("x_tail_set")
        weight_turned = sem("weight_turned")
        weight_copied = sem("weight_copied")
        oh_built = sem("oh_built")
        oh_counted = sem("oh_counted")
        setup_pe = sem("setup_pe")
        setup_dve = sem("setup_dve")
        rows_of_chunk = sem("rows_of_chunk")
        vec = sem("vec")
        rows_in = [sem(f"rows_in{j}") for j in range(U)]
        idx_copied = sem("idx_copied")
        onehot_ready = sem("onehot_ready")
        sums_ready = sem("sums_ready")
        sums_added = sem("sums_added")
        rows_used = sem("rows_used")
        table_out = sem("table_out")
        root_asked = sem("root_asked")
        root_taken = sem("root_taken")
        x_ready = sem("x_ready")
        tail_set = sem("tail_set")
        kv_out = [sem(f"kv_out{u}") for u in range(2)]
        qkv_in = sem("qkv_in")
        ot_turned = sem("ot_turned")
        ot_copied = sem("ot_copied")
        scores_done = sem("scores_done")
        hs_s = sem("hs_s")
        hs_d = sem("hs_d")
        hs_turned = sem("hs_turned")
        hs_run = sem("hs_run")
        hs_done = sem("hs_done")
        hs_back = sem("hs_back")
        hs_out = sem("hs_out")
        sweep_ready = sem("sweep_ready")
        sweep_max = sem("sweep_max")
        expand_ready = sem("expand_ready")
        weights_minus = sem("weights_minus")
        weights_ready = sem("weights_ready")
        acc_zero = sem("acc_zero")
        parts_set = sem("parts_set")
        parts_joined = sem("parts_joined")
        ffn_in = sem("ffn_in")
        h_product = sem("h_product")
        h_done = sem("h_done")
        y_ready = sem("y_ready")
        src_turned = sem("src_turned")
        src_rows_ready = sem("src_rows_ready")
        hi_rows_set = sem("hi_rows_set")
        hi_rows_out = sem("hi_rows_out")
        hi_in = [sem(f"hi_in{b}") for b in range(2)]
        tile_onehot_built = sem("tile_onehot_built")
        row_looked_up = sem("row_looked_up")
        src_taken = sem("src_taken")
        tile_onehots_asked = sem("tile_onehots_asked")
        xp_out = sem("xp_out")
        src_copied = sem("src_copied")
        src_up = sem("src_up")
        least_step = sem("least_step")
        least_turned = sem("least_turned")
        self_ready = sem("self_ready")
        scaled_ready = sem("scaled_ready")
        gates_ready = sem("gates_ready")
        cell_ready = sem("cell_ready")
        cell_tanh = sem("cell_tanh")
        gathers_asked = sem("gathers_asked")
        transposes_asked = sem("transposes_asked")
        d_pre = sem("d_pre")
        d_turned = sem("d_turned")
        d_evac = sem("d_evac")
        d_product = sem("d_product")
        d_post = sem("d_post")
        pass_init = sem("pass_init")
        out_done = sem("out_done")

        block = ctx.enter_context(nc.Block())

        n_weights = [0]

        def setup_sync(sp):
            sp.dma_start(dst_i, a["dst"].rearrange("(p c) -> p c", p=EP)).then_inc(dst_in, 16)
            full = (CHUNKS - 1) * P
            for k, name in enumerate(("src", "dst")):
                sp.dma_start(edges_d[0:CHUNKS - 1, k * P:(k + 1) * P],
                             a[name][0:full].rearrange("(c e) -> c e", e=P)).then_inc(edges_in, 16)
                sp.dma_start(edges_d[CHUNKS - 1:CHUNKS, k * P:k * P + E - full],
                             a[name][full:E].rearrange("(c e) -> c e", c=1)).then_inc(edges_in, 16)
            for o, name in enumerate(("L1_gnn_W", "L3_gnn_W")):
                sp.dma_start((nat_L1, nat_L3)[o], a[name].rearrange("(o p) d -> p o d", p=P)).then_inc(natural_in, 16)
            for g, row in enumerate((0, 2 * D, 3 * D)):
                sp.dma_start(nat_ih[:, 2 * g:2 * g + 2, :],
                             a["L3_gnn_W_ih"][row:row + D, :].rearrange("(o p) d -> p o d", p=P)).then_inc(natural_in, 16)
            for k, name in enumerate(("L3_gnn_att_src", "L3_gnn_att_dst")):
                sp.dma_start(att[:, 2 * k:2 * k + 2], a[name].rearrange("(o p) -> p o", p=P),
                             allow_slow_non_contiguous=True).then_inc(natural_in, 16)
            full_t = N // P
            sp.dma_start(X[:, 0:full_t * D].rearrange("p (t d) -> p t d", d=D),
                         a["x"][0:full_t * P, :].rearrange("(t p) d -> p t d", p=P)).then_inc(x_in, 16)
            loads = [(W1, a["L0_gnn_W1"].rearrange("(k p) n -> p k n", p=P)),
                     (W2[:, :], a["L0_gnn_W2"]), (W3[:, :], a["L0_gnn_W3"]), (W4[:, :], a["L0_gnn_W4"]),
                     (W5[:, :], a["L0_gnn_W5"]), (W6, a["L0_gnn_W6"]),
                     (Wo[:, :, :], a["L2_gnn_Wo_w"].rearrange("(k p) n -> p k n", p=P)),
                     (fb1[:, :], a["L2_gnn_ffn_b1"].rearrange("(f p) -> p f", p=P))]
            for dst, src in loads:
                sp.dma_start(dst, src, allow_slow_non_contiguous=True).then_inc(weights_in, 16)
            for name, w in BIAS_W.items():
                sp.dma_start(bias[name][:, :], a[name].rearrange("(o d) -> o d", o=1).to_broadcast([P, w])
                             ).then_inc(bias_in, 16)
            sp.wait_ge(x_tail_set, 1)
            sp.dma_start(X[0:N - full_t * P, full_t * D:(full_t + 1) * D], a["x"][full_t * P:N, :]).then_inc(x_in, 16)
            sp.wait_ge(pads_set, 2)
            sp.dma_start(edges_d[CHUNKS - 1:CHUNKS, E - full:P], pad_i[0:1, E - full:P]).then_inc(edges_padded, 16)
            sp.dma_start(edges_d[CHUNKS - 1:CHUNKS, P + E - full:2 * P], pad_i[0:1, P + E - full:2 * P]).then_inc(edges_padded, 16)
            sp.dma_start(edges_d[CHUNKS:CROWS, :], pad_i).then_inc(edges_padded, 16)
            sp.wait_ge(hi_rows_set, 1)
            sp.dma_start(hi_rows.rearrange("(k p) e -> p k e", p=P), hi_b_rows).then_inc(hi_rows_out, 16)
            sp.wait_ge(hi_rows_out, 16)

        def setup_pool(pool):
            pool.memset(X[:, (TILES - 1) * D:TP * D], 0.0).then_inc(x_tail_set, 1)
            pool.memset(pad_i[:, 0:P], 0).then_inc(pads_set, 1)
            pool.memset(pad_i[:, P:2 * P], NO_NODE).then_inc(pads_set, 1)
            pool.iota(viota_i, [[1, VT]], base=0, channel_multiplier=0).then_inc(consts_set, 1)
            pool.iota(small[:, 0:VB].bitcast(I32), [[P, VB]], base=0, channel_multiplier=1).then_inc(consts_set, 1)
            pool.iota(small[:, 16:17].bitcast(I32), [[1, 1]], base=0, channel_multiplier=1).then_inc(consts_set, 1)
            pool.memset(ident[:, :], 0.0).then_inc(consts_set, 1)
            pool.memset(ones[:, :], 1.0).then_inc(consts_set, 1)
            pool.memset(zero_b, 0.0).then_inc(consts_set, 1)
            pool.wait_ge(consts_set, 6)
            pool.affine_select(out=ident[:, :], in_=ident[:, :], compare_op=ALU.not_equal, fill=1.0, base=0,
                               pattern=[[-1, P + 1]], channel_multiplier=1).then_inc(consts_set, 1)
            pool.affine_select(out=tri, in_=ones[:, :], compare_op=ALU.is_ge, fill=0.0, base=0,
                               pattern=[[1, P]], channel_multiplier=-1).then_inc(consts_set, 1)
            pool.wait_ge(edges_in, 64)
            pool.wait_ge(edges_padded, 48)
            pool.wait_ge(setup_dve, 5)
            for k in range(VB):
                nc.gpsimd.indirect_dma_start(edge_i[:, k, :], None, edges_d,
                                             bass.IndirectOffsetOnAxis(small[:, 48 + k:49 + k].bitcast(I32), 0)
                                             ).then_inc(rows_of_chunk, 16)

        nat_blocks = ([(L1T[:, db, ob * P:(ob + 1) * P], nat_L1[:, ob, db * P:(db + 1) * P]) for db in range(2) for ob in range(2)]
                      + [(L3T[:, db, ob * P:(ob + 1) * P], nat_L3[:, ob, db * P:(db + 1) * P]) for db in range(2) for ob in range(2)]
                      + [(WihT[:, db, ob * P:(ob + 1) * P], nat_ih[:, ob, db * P:(db + 1) * P]) for db in range(2) for ob in range(6)])

        def setup_tensor(pe):
            pe.sem_inc(sums_ready, U)
            pe.sem_inc(oh_counted, 2)
            pe.sem_inc(d_turned, 2)
            pe.sem_inc(d_product, 2)
            pe.sem_inc(hs_turned, 1)
            pe.wait_ge(consts_set, 8)
            pe.wait_ge(natural_in, 16 * 7)
            for n, (_, src) in enumerate(nat_blocks):
                if n >= 2:
                    pe.wait_ge(weight_copied, n - 1)
                pe.transpose(bank[n % 2][:, 0:P], src, ident[:, 0:P]).then_inc(weight_turned, 1)
            for db in range(2):
                for k in range(2):
                    for ob in range(2):
                        m = pe.matmul(bank[2][:, 2 * db + k:2 * db + k + 1], nat_L3[:, ob, db * P:(db + 1) * P],
                                      att[:, 2 * k + ob:2 * k + ob + 1], start=(ob == 0), stop=(ob == 1))
            m.then_inc(weight_turned, 1)
            pe.matmul(bank[3][0:TILES, 0:P], zero_b[:, 0:TILES], zero_b, start=True, stop=False, skip_group_check=True)
            with pe.Fori(0, EC // U // 2) as i:
                for b in range(2):
                    pe.wait_ge(oh_built, i * 4 + 2 * b + 2)
                    for c in range(U):
                        m = pe.matmul(bank[3][0:TILES, 0:P], oh_hi[:, b, c, :], oh_lo[:, b, c, :], start=False, stop=False,
                                      skip_group_check=True)
                    m.then_inc(oh_counted, 1)
            pe.matmul(bank[3][0:TILES, 0:P], zero_b[:, 0:TILES], zero_b, start=False, stop=True,
                      skip_group_check=True).then_inc(setup_pe, 1)
            pe.wait_ge(setup_dve, 2)
            pe.transpose(bank[4][:, 0:TILES], hist, ident[0:TILES, 0:TILES]).then_inc(setup_pe, 1)
            pe.matmul(bank[5][0:TILES - 1, 0:1], tri[0:TILES, 0:TILES - 1], small[0:TILES, 20:21], start=True,
                      stop=True).then_inc(setup_pe, 1)
            pe.wait_ge(setup_dve, 4)
            for k in range(VB):
                m = pe.matmul(bank[6][:, k:k + 1], passed[:, k * P:(k + 1) * P], ones[0:TILES - 1, 0:1], start=True, stop=True)
            m.then_inc(setup_pe, 1)
            for k in range(2):
                m = pe.matmul(bank[4 + k][:, 0:VT // 2], ones[0:TILES - 1, :], passed[:, k * (VT // 2):(k + 1) * (VT // 2)],
                              start=True, stop=True)
            m.then_inc(setup_pe, 1)
            pe.wait_ge(setup_dve, 6)
            for k in range(VB):
                for s in range(2):
                    b = 2 * (k % 2) + s
                    if k >= 2:
                        pe.wait_ge(setup_dve, 7 + 2 * (k - 2) + s)
                    elif k == 1 and s == 1:
                        pass
                    pe.transpose(bank[b][:, 0:P], edge_f[:, k, s * P:(s + 1) * P], ident[:, 0:P]).then_inc(setup_pe, 1)
            pe.wait_ge(setup_dve, 6 + 2 * VB)
            for k in range(2):
                m = pe.matmul(bank[4 + k][:, 0:VT // 2], ident[:, 1:P + 1], dloc[:, k * (VT // 2):(k + 1) * (VT // 2)],
                              start=True, stop=True)
            m.then_inc(setup_pe, 1)

        def setup_scalar(act):
            act.sem_inc(d_evac, 2)
            act.sem_inc(ot_copied, 2)
            act.sem_inc(src_copied, 2)
            act.sem_inc(h_done, 2)
            act.sem_inc(gates_ready, 2)
            for n, (dst, _) in enumerate(nat_blocks):
                act.wait_ge(weight_turned, n + 1)
                act.copy(dst, bank[n % 2][:, 0:P]).then_inc(weight_copied, 1)
            act.wait_ge(weight_turned, len(nat_blocks) + 1)
            act.copy(L3T[:, :, D:D + 2], bank[2][:, 0:4].rearrange("p (b k) -> p b k", b=2)).then_inc(weight_copied, 1)

        roots = [0, 0]

        def inverse_root(v, st, x, tmp, n):
            y = tmp2[:, 0:n]
            v.sem_inc(root_asked, 1)
            roots[0] += 1
            v.wait_ge(root_taken, roots[0])
            st.link(v.reciprocal(tmp, tmp))
            st.link(v.tensor_tensor(y, tmp, tmp, ALU.mult))
            st.link(v.tensor_tensor(y, y, x, ALU.mult))
            st.link(v.tensor_scalar(y, y, -0.5, 1.5, ALU.mult, ALU.add))
            st.link(v.tensor_tensor(x, y, tmp, ALU.mult))

        def take_root(act, x, tmp):
            roots[1] += 1
            act.wait_ge(root_asked, roots[1])
            act.activation(tmp, x, ACT.Sqrt).then_inc(root_taken, 1)

        def setup_vector(v, st):
            v.sem_inc(sums_added, SUM_BANKS)
            v.sem_inc(rows_used, U)
            v.sem_inc(d_post, 2)
            v.sem_inc(sweep_max, U)
            v.sem_inc(weights_minus, 2)
            v.memset(S[:, VISITS * HEADS:], 0.0).then_inc(tail_set, 1)
            v.wait_ge(consts_set, 8)
            st.link(v.tensor_copy(viota, viota_i))
            st.link(v.tensor_copy(small[:, 8:8 + VB], small[:, 0:VB].bitcast(I32)))
            st.link(v.tensor_copy(small[:, 17:18], small[:, 16:17].bitcast(I32)))
            st.link(v.tensor_copy(iota[:, :], viota[:, 0:P]))
            st.link(v.tensor_copy(iota_b, iota[:, :]))
            v.wait_ge(dst_in, 16)
            st.link(v.tensor_scalar(hi_i, dst_i, 7, None, ALU.arith_shift_right))
            st.link(v.tensor_scalar(lo_i, dst_i, P - 1, None, ALU.bitwise_and))
            st.link(v.tensor_copy(hi_f, hi_i))
            st.link(v.tensor_copy(lo_f, lo_i))
            with v.Fori(0, EC // U // 2) as i:
                for b in range(2):
                    v.wait_ge(oh_counted, i * 2 + (b + 1))
                    v.tensor_tensor(oh_lo[:, b], iota_b[0:EP, :].unsqueeze(1).to_broadcast([EP, U, P]),
                                    lo_f[:, ds(i * (2 * U) + b * U, U)].unsqueeze(2).to_broadcast([EP, U, P]),
                                    ALU.is_equal).then_inc(oh_built, 1)
                    v.tensor_tensor(oh_hi[:, b], iota_b[0:EP, 0:TILES].unsqueeze(1).to_broadcast([EP, U, TILES]),
                                    hi_f[:, ds(i * (2 * U) + b * U, U)].unsqueeze(2).to_broadcast([EP, U, TILES]),
                                    ALU.is_equal).then_inc(oh_built, 1)
            v.wait_ge(setup_pe, 1)
            v.tensor_copy(hist, bank[3][0:TILES, 0:P]).then_inc(setup_dve, 1)
            v.wait_ge(setup_dve, 1)
            v.tensor_reduce(small[0:TILES, 20:21], hist, AX.X, ALU.add).then_inc(setup_dve, 1)
            v.wait_ge(setup_pe, 2)
            st.link(v.memset(dis[:, :], 1.0))
            st.link(v.tensor_scalar(dis[:, 0:TILES], bank[4][:, 0:TILES], 1.0, None, ALU.add))
            inverse_root(v, st, dis[:, 0:TILES], root[:, 0:TILES], TILES)
            v.wait_ge(setup_pe, 3)
            pos = small[0:TILES - 1, 21:22].bitcast(I32)
            st.link(v.tensor_copy(pos, bank[5][0:TILES - 1, 0:1]))
            st.link(v.tensor_scalar(small[0:TILES - 1, 22:23].bitcast(I32), pos, 7, None, ALU.arith_shift_right))
            st.link(v.tensor_copy(small[0:TILES - 1, 23:24], small[0:TILES - 1, 22:23].bitcast(I32)))
            v.tensor_tensor(small[0:TILES - 1, 24:25], small[0:TILES - 1, 23:24], small[0:TILES - 1, 17:18],
                            ALU.add).then_inc(setup_dve, 1)
            v.wait_ge(setup_dve, 3)
            v.tensor_scalar(passed, viota[0:TILES - 1, :], small[0:TILES - 1, 24:25], None, ALU.is_gt).then_inc(setup_dve, 1)
            v.wait_ge(setup_pe, 4)
            st.link(v.tensor_tensor(small[:, 32:32 + VB], small[:, 8:8 + VB], bank[6][:, 0:VB], ALU.subtract))
            v.tensor_scalar(small[:, 48:48 + VB].bitcast(I32), small[:, 32:32 + VB], float(CROWS - 1), None,
                            ALU.min).then_inc(setup_dve, 1)
            v.wait_ge(setup_pe, 5)
            h = VT // 2
            for k in range(2):
                st.link(v.tensor_copy(tile_of[:, k * h:(k + 1) * h], bank[4 + k][0:1, 0:h]))
            for k in range(2):
                st.link(v.tensor_scalar(dnext[:, k * h:(k + 1) * h], bank[4 + k][:, 0:h], float(P), None, ALU.mult))
            v.wait_ge(rows_of_chunk, 16 * VB)
            v.tensor_copy(edge_f, edge_i).then_inc(setup_dve, 1)
            st.link(v.tensor_scalar(hi_i_rows, edge_i[:, :, 0:P], 7, None, ALU.arith_shift_right))
            v.tensor_copy(hi_b_rows, hi_i_rows).then_inc(hi_rows_set, 1)
            for k in range(VB):
                v.wait_ge(setup_pe, 5 + 2 * k + 1)
                v.tensor_copy(idx_tab[:, k * P:(k + 1) * P], bank[2 * (k % 2)][:, 0:P]).then_inc(setup_dve, 1)
                v.wait_ge(setup_pe, 5 + 2 * k + 2)
                v.tensor_tensor(dloc[:, k * P:(k + 1) * P], bank[2 * (k % 2) + 1][:, 0:P], dnext[:, k * P:(k + 1) * P],
                                ALU.subtract).then_inc(setup_dve, 1)
            v.wait_ge(setup_dve, 6 + 2 * VB)
            v.wait_ge(setup_pe, 6 + 2 * VB)
            st.link(v.tensor_scalar(small[:, 25:26], small[:, 17:18], float(P - 1), None, ALU.is_equal))
            for k in range(2):
                st.link(v.tensor_tensor(dnext[:, k * h:(k + 1) * h], bank[4 + k][:, 0:h], dloc[:, k * h:(k + 1) * h],
                                        ALU.not_equal))
            st.link(v.tensor_scalar(dnext, dnext, small[:, 25:26], None, ALU.max))
            st.link(v.tensor_scalar(dlast[:, :], dloc[:, :], 1.0, None, ALU.add))
            st.link(v.tensor_tensor(dlast[:, :], dlast[:, :], dnext, ALU.mult))
            st.link(v.tensor_scalar(dlast[:, :], dlast[:, :], -1.0, None, ALU.add))

        def copy_indices(eng, i, h, used, base, on_scalar=False):
            eng.wait_ge(used, i * U + (base + h * HALF + HALF))
            copy = eng.copy if on_scalar else eng.tensor_copy
            copy(idx_now[:, h * HALF:(h + 1) * HALF], idx_tab[:, ds(i * U + h * HALF, HALF)]).then_inc(idx_copied, 1)

        def indices_scalar(act, used, base):
            with act.Fori(0, TURNS) as i:
                for h in range(2):
                    copy_indices(act, i, h, used, base, True)

        def gather_rows(pool, g, table, w, used, base, stored, stored_sem=table_out, own_indices=True):
            pool.wait_ge(stored_sem, stored)
            with pool.Fori(0, TURNS) as i:
                for h in range(2):
                    if own_indices:
                        copy_indices(pool, i, h, used, base)
                    pool.wait_ge(idx_copied, i * 2 + (g * 2 * TURNS + h + 1))
                    pool.sem_inc(gathers_asked, 1)
                    for j in range(h * HALF, (h + 1) * HALF):
                        nc.gpsimd.indirect_dma_start(ring[:, j, 0:w], None, table,
                                                     bass.IndirectOffsetOnAxis(idx_now[:, j:j + 1], 0)
                                                     ).then_inc(rows_in[j], 16)

        def load_tiles(eng, regs, i, lo, n):
            eng.load(regs[0:n], tile_of[0:1, ds(i * U + lo, n)])
            return [eng.snap(r, min_val=0, max_val=TILES - 1) for r in regs[0:n]]

        def sum_tensor(pe, p, g, m, oh_base):
            w = widths[p]
            with pe.Fori(0, TURNS) as i:
                for j in range(U):
                    pe.wait_ge(rows_in[j], i * 16 + 16 * (g * TURNS + 1))
                    pe.wait_ge(onehot_ready, i * U + (oh_base + j + 1))
                    pe.wait_ge(sums_added, i * U + (m * VISITS + j + 1))
                    pe.matmul(bank[SBANK + j % SUM_BANKS][:, 0:w], onehot[:, j, :], ring[:, j, 0:w], start=True,
                              stop=True).then_inc(sums_ready, 1)

        def build_onehot(v, i, j, ahead, table=None):
            v.tensor_scalar(onehot[:, (j + ahead) % U, :], iota[:, :], (dloc if table is None else table)[:, ds(i * U + j + ahead, 1)],
                            None, ALU.is_equal).then_inc(onehot_ready, 1)

        def sum_vector(v, p, m, regs):
            w = widths[p]
            for j in range(HALF):
                build_onehot(v, 0, j, 0)
            with v.Fori(0, TURNS) as i:
                tile = load_tiles(v, regs, i, 0, U)
                for j in range(U):
                    build_onehot(v, i, j, HALF)
                    v.wait_ge(sums_ready, i * U + (U + m * VISITS + j + 1))
                    v.wait_ge(sums_added, i * U + (SUM_BANKS + m * VISITS + j))
                    acc = acc_tile(p, tile[j])
                    v.tensor_tensor(acc, acc, bank[SBANK + j % SUM_BANKS][:, 0:w], ALU.add).then_inc(sums_added, 1)

        def by_pairs(eng, body, st=None, per=0):
            with eng.Fori(0, TP // 2 - 1) as i:
                if st is not None:
                    st.enter(i, per)
                body(i * 2, False)
                if st is not None:
                    st.leave(TP // 2 - 1)
            body(TP - 2, True)

        def dense_turn(pe, q, w_in, t, u):
            kb = -(-w_in // P)
            kw = min(w_in, P)
            pe.wait_ge(d_pre, t + (q * TP + 1))
            pe.wait_ge(d_evac, t + (q * TP + 1))
            if kw == 64:
                pe.sem_inc(transposes_asked, 1)
            for k in range(kb):
                m = pe.transpose(bank[u][0:kw, k * P:(k + 1) * P], pre[:, u, k * kw:(k + 1) * kw], ident[:, 0:P])
            m.then_inc(d_turned, 1)

        def dense_tensor(pe, q, w_in, weights, w_out, read_out=None):
            kb = -(-w_in // P)
            kw = min(w_in, P)

            def body(t, last):
                for u in range(2):
                    if not (last and u):
                        dense_turn(pe, q, w_in, t + (u + 1), 1 - u)
                    pe.wait_ge(d_evac, t + (q * TP + u + 3))
                    if read_out is None:
                        pe.wait_ge(d_post, t + (q * TP + u + 1))
                    else:
                        pe.wait_ge(read_out, t + (u + 1))
                    for n, wt in enumerate(weights):
                        for k in range(kb):
                            m = pe.matmul(bank[2 + u + 2 * (n // 2)][:, (n % 2) * w_out:(n % 2 + 1) * w_out],
                                          turned[0:kw, u, k, :], wt(k), start=(k == 0), stop=(k == kb - 1))
                    m.then_inc(d_product, 1)

            if read_out is not None:
                pe.wait_ge(d_post, q * TP + 2)
            dense_turn(pe, q, w_in, 0, 0)
            by_pairs(pe, body)

        def bring(eng, q, src, w, given=None, base=0):
            with eng.Fori(0, TP // 2) as i:
                for u in range(2):
                    eng.wait_ge(d_turned, i * 2 + (q * TP + u + 1))
                    if given is not None:
                        eng.wait_ge(given, i * 2 + (base + u + 1))
                    eng.tensor_copy(pre[:, u, 0:w], src(i * 2 + u)).then_inc(d_pre, 1)

        def evacuate(act, q, w_in, func, t, u):
            kb = -(-w_in // P)
            kw = min(w_in, P)
            act.wait_ge(d_turned, t + (q * TP + 3))
            act.activation(turned[0:kw, u, 0:kb, :], bank[u][0:kw, 0:kb * P].rearrange("p (k n) -> p k n", k=kb),
                           func).then_inc(d_evac, 1)

        def dense_scalar(act, q, w_in, func):
            with act.Fori(0, TP // 2) as i:
                for u in range(2):
                    act.wait_ge(d_product, i * 2 + (q * TP + u + 1))
                    evacuate(act, q, w_in, func, i * 2 + u, u)

        def table_sync(sp, done, base, table, w, off, sem_out):
            with sp.Fori(0, TP // 2) as i:
                sp.wait_ge(done, i * 2 + (base + 2))
                sp.dma_start(table[ds(i * 2 * P, 2 * P), :].rearrange("(t p) d -> p t d", p=P),
                             ACC[:, ds(i * 2 * w + off, 2 * w)].rearrange("p (t d) -> p t d", t=2)).then_inc(sem_out, 16)

        def acc_of(p):
            return lambda t: acc_tile(p, t)

        def x_of(t):
            return X[:, ds(t * D, D)]

        def col(tab, t, w=1):
            return tab[:, ds(t * w, w)]

        def norm_factors(v, st):
            even, odd = moments[:, :, 1], moments[:, :, 4]
            st.link(v.tensor_tensor(mean[:, :], even, odd, ALU.add))
            st.link(v.tensor_scalar(mean[:, :], mean[:, :], 0.5, None, ALU.mult))
            st.link(v.tensor_tensor(root[:, :], even, mean[:, :], ALU.subtract))
            st.link(v.tensor_tensor(root[:, :], root[:, :], root[:, :], ALU.mult))
            st.link(v.tensor_tensor(rstd[:, :], moments[:, :, 2], moments[:, :, 5], ALU.add))
            st.link(v.scalar_tensor_tensor(out=rstd[:, :], in0=rstd[:, :], scalar=1.0 / D, in1=root[:, :],
                                           op0=ALU.mult, op1=ALU.add))
            st.link(v.tensor_scalar(rstd[:, :], rstd[:, :], EPS, None, ALU.add))
            inverse_root(v, st, rstd[:, :], root[:, :], TP)
            st.link(v.scalar_tensor_tensor(out=shift[:, :], in0=mean[:, :], scalar=-1.0, in1=rstd[:, :],
                                           op0=ALU.mult, op1=ALU.mult))

        def after(v, st, q, per, post, pre_=None):
            def body(t, last):
                for u in range(2):
                    if pre_ is not None and not last:
                        v.wait_ge(d_turned, t + (q * TP + u + 3))
                        pre_(t + (u + 2), u)
                    v.wait_ge(d_product, t + (q * TP + u + 3))
                    post(t + u, u)

            if pre_ is not None:
                v.wait_ge(d_turned, q * TP + 2)
                pre_(0, 0)
                pre_(1, 1)
            by_pairs(v, body, st, per)

        def scaled_layer_in(v, p, bname):
            w = widths[p]

            def f(t, u):
                v.scalar_tensor_tensor(out=pre[:, u, 0:w], in0=acc_tile(p, t), scalar=col(dis, t), in1=bias[bname][:, :],
                                       op0=ALU.mult, op1=ALU.add).then_inc(d_pre, 1)
            return f

        def product_scaled(v, p):
            def f(t, u):
                v.tensor_scalar(acc_tile(p, t), bank[2 + u][:, 0:widths[p]], col(dis, t), None, ALU.mult).then_inc(d_post, 1)
            return f

        def product_biased(v, st, p, bname):
            w = widths[p]

            def f(t, u):
                st.link(v.scalar_tensor_tensor(out=mid[:, u, 0:w], in0=bank[2 + u][:, 0:w], scalar=col(dis, t),
                                               in1=bias[bname][:, :], op0=ALU.mult, op1=ALU.add))
                v.tensor_scalar(acc_tile(p, t), mid[:, u, 0:w], 0.0, col(dis, t), ALU.max, ALU.mult).then_inc(d_post, 1)
            return f

        def residual_in(v, st, bname, relu):
            def f(t, u):
                st.link(v.scalar_tensor_tensor(out=mid[:, u, :], in0=bank[2 + u][:, 0:D], scalar=col(dis, t),
                                               in1=bias[bname][:, :], op0=ALU.mult, op1=ALU.add))
                if relu:
                    st.link(v.tensor_scalar(mid[:, u, :], mid[:, u, :], 0.0, None, ALU.max))
                st.link(v.tensor_tensor(x_of(t), mid[:, u, :], x_of(t), ALU.add))
                v.bn_stats(col(moments[:, :, :].rearrange("p t s -> p (t s)"), t, 6), x_of(t)).then_inc(d_post, 1)
            return f

        def norm_x(v, st, q):
            v.wait_ge(d_post, q * TP + 2)
            norm_factors(v, st)
            with v.Fori(0, TP // 2) as i:
                for u in range(2):
                    t = i * 2 + u
                    v.tensor_scalar(x_of(t), x_of(t), col(rstd, t), col(shift, t), ALU.mult, ALU.add).then_inc(x_ready, 1)

        def scale_rows(act, p, sem_done):
            with act.Fori(0, TP // 2) as i:
                for u in range(2):
                    t = i * 2 + u
                    act.wait_ge(x_ready, t + 1)
                    act.activation(acc_tile(p, t), x_of(t), ACT.Copy, scale=col(dis, t)).then_inc(sem_done, 1)

        def twice_scaled(v, st, p, bname, sem_done):
            w = widths[p]
            with v.Fori(0, TP // 2) as i:
                st.enter(i, 2)
                for u in range(2):
                    t = i * 2 + u
                    st.link(v.scalar_tensor_tensor(out=mid[:, u, 0:w], in0=acc_tile(p, t), scalar=col(dis, t),
                                                   in1=bias[bname][:, :], op0=ALU.mult, op1=ALU.add))
                    v.tensor_scalar(acc_tile(p, t), mid[:, u, 0:w], col(dis, t), None, ALU.mult).then_inc(sem_done, 1)
                st.leave(TP // 2)

        OH_SUM = VISITS + HALF
        OH_TWO = VISITS + U
        OT_PASS = 2 * (2 * TURNS + 1)
        h3_done = sem("h3_done")
        t7_done = sem("t7_done")

        TURN_AT = (1, 2)

        def turn_onehots(pe, i, h, o, r, hh, four=(0, 1)):
            for q in four:
                pe.wait_ge(onehot_ready, i * U + (o + h * HALF + 4 * q + 4))
                pe.wait_ge(ot_copied, i * 4 + (r * OT_PASS + 2 * h + q + 1))
                for c in range(4):
                    t = pe.transpose(bank[q][:, c * P:(c + 1) * P], onehot[:, hh * HALF + 4 * q + c, :], ident[:, 0:P])
                t.then_inc(ot_turned, 1)

        def copy_turned(act, i, h, r, m, hh):
            for q in range(2):
                act.wait_ge(ot_turned, i * 4 + (r * OT_PASS + 2 * h + q + 1))
                act.wait_ge(sums_ready, i * U + (m * VISITS + h * HALF + HALF))
                act.copy(onehotT[:, hh, 4 * q:4 * q + 4, :], bank[q][:, :].rearrange("p (c n) -> p c n", c=4)
                         ).then_inc(ot_copied, 1)

        def score_tensor(pe, o, r, m, regs):
            turn_onehots(pe, 0, 0, o, r, 0)
            with pe.Fori(0, TURNS) as i:
                for h in range(2):
                    tile = load_tiles(pe, regs, i, h * HALF, HALF)
                    for j in range(HALF):
                        if j in TURN_AT:
                            turn_onehots(pe, i, h + 1, o, r, 1 - h, (TURN_AT.index(j),))
                        if j % 4 == 0:
                            pe.wait_ge(ot_copied, i * 4 + (r * OT_PASS + 2 * h + j // 4 + 3))
                        pe.wait_ge(rows_used, i * U + (h * HALF + j + U - 3))
                        pe.matmul(bank[SBANK + j % SUM_BANKS][:, 0:D], onehotT[:, h, j, :],
                                  ACC[:, ds(tile[j] * D, D)], start=True, stop=True).then_inc(sums_ready, 1)

        def score_scalar(act, r, m):
            copy_turned(act, 0, 0, r, m, 0)
            with act.Fori(0, TURNS) as i:
                for h in range(2):
                    copy_indices(act, i, h, rows_used, 0, True)
                    copy_turned(act, i, h + 1, r, m, 1 - h)

        def score_vector(v, g, m):
            for j in range(U):
                build_onehot(v, 0, j, 0)
            with v.Fori(0, TURNS) as i:
                for j in range(U):
                    v.wait_ge(sums_ready, i * U + (U + m * VISITS + j + 1))
                    v.wait_ge(rows_in[j], i * 16 + 16 * (g * TURNS + 1))
                    v.tensor_tensor(message[:, j % 2, :], bank[SBANK + j % SUM_BANKS][:, 0:D], ring[:, j, 0:D],
                                    ALU.mult).then_inc(rows_used, 1)
                    build_onehot(v, i, j, U)
                    v.wait_ge(rows_used, i * U + (U + j + 1))
                    v.tensor_reduce(S[:, ds(i * (U * HEADS) + j * HEADS, HEADS)],
                                    message[:, j % 2, :].rearrange("p (h d) -> p h d", h=HEADS), AX.X,
                                    ALU.add).then_inc(scores_done, 1)

        def running_max(v, st, run_, dst_, tmp_):
            k = 1
            while k < P:
                st.link(v.tensor_tensor(tmp_[:, :, k:P], dst_[:, :, k:P], dst_[:, :, 0:P - k], ALU.is_equal))
                st.link(v.tensor_tensor(tmp_[:, :, k:P], tmp_[:, :, k:P], run_[:, :, 0:P - k], ALU.mult))
                st.link(v.tensor_tensor(run_[:, :, k:P], run_[:, :, k:P], tmp_[:, :, k:P], ALU.max))
                k *= 2

        def blocks(x):
            return x.rearrange("p (b n) -> p b n", n=P)

        GROUP = 4 * P // HEADS
        GROUPS = VISITS // GROUP

        def segment_tensor(pe):
            with pe.Fori(0, GROUPS) as g:
                pe.wait_ge(hs_s, g + 1)
                pe.wait_ge(hs_d, g + 1)
                for b in range(4):
                    pe.transpose(bank[0][:, b * P:(b + 1) * P], st_s[:, b * P:(b + 1) * P], ident[:, 0:P])
                for b in range(4):
                    t = pe.transpose(bank[1][:, b * P:(b + 1) * P], st_d[:, b * P:(b + 1) * P], ident[:, 0:P])
                t.then_inc(hs_turned, 1)
                pe.wait_ge(hs_done, g + 1)
                for b in range(4):
                    t = pe.transpose(bank[2][:, b * P:(b + 1) * P], run[:, b * P:(b + 1) * P], ident[:, 0:P])
                t.then_inc(hs_back, 1)

        def segment_scalar(act):
            act.wait_ge(scores_done, VISITS)
            with act.Fori(0, GROUPS) as g:
                act.copy(st_s, S[:, ds(g * 512, 512)]).then_inc(hs_s, 1)
                act.wait_ge(hs_turned, g + 2)
                act.copy(run, bank[0][:, :]).then_inc(hs_run, 1)
                act.wait_ge(hs_back, g + 1)
                act.copy(ACC[:, ds(g * 512, 512)], bank[2][:, :]).then_inc(hs_out, 1)

        def segment_pool(pool):
            pool.wait_ge(scores_done, VISITS)
            with pool.Fori(0, GROUPS) as g:
                pool.wait_ge(hs_turned, g + 1)
                pool.tensor_copy(st_d.rearrange("p (v h) -> p v h", h=HEADS),
                                 dloc[:, ds(g * GROUP, GROUP)].unsqueeze(2).to_broadcast([P, GROUP, HEADS])
                                 ).then_inc(hs_d, 1)

        def segment_vector(v, st):
            with v.Fori(0, GROUPS) as g:
                st.enter(g, 22)
                v.wait_ge(hs_run, g + 1)
                st.link(v.tensor_copy(run_dst, bank[1][:, :]))
                running_max(v, st, blocks(run), blocks(run_dst), blocks(run_tmp))
                v.tensor_copy(small[:, 30:31], run[:, 0:1]).then_inc(hs_done, 1)
                st.leave(GROUPS)

        def sweep_tensor(pe, o, s, w, src):
            with pe.Fori(0, TURNS) as i:
                for h in range(2):
                    pe.wait_ge(sweep_max, i * U + (s * VISITS + h * HALF + HALF))
                    for j in range(HALF):
                        pe.wait_ge(onehot_ready, i * U + (o + h * HALF + j + 1))
                        t = pe.matmul(bank[h][:, j * w:(j + 1) * w], onehot[:, h * HALF + j, :],
                                      src[:, ds(i * (U * w) + (h * HALF + j) * w, w)], start=True, stop=True)
                    t.then_inc(sweep_ready, 1)

        def sweep_vector(v, s, w, dst, regs):
            part = [dst[:, 0:TP * w]] + [ringf[:, 2560 + k * TP * HEADS:2560 + k * TP * HEADS + TP * w] for k in range(3)]
            for k in range(1, 4):
                v.memset(part[k], 0.0).then_inc(parts_set, 1)
            v.wait_ge(parts_set, 3 * (s + 1))
            for j in range(HALF):
                build_onehot(v, 0, j, 0, dlast)
            with v.Fori(0, TURNS) as i:
                tile = load_tiles(v, regs, i, 0, U)
                for h in range(2):
                    for j in range(HALF):
                        build_onehot(v, i, h * HALF + j, HALF, dlast)
                    v.wait_ge(sweep_ready, i * 2 + (s * 2 * TURNS + h + 1))
                    for j in range(HALF):
                        v.wait_ge(sweep_max, i * U + (U + s * VISITS + h * HALF + j - 3))
                        m = part[j % 4][:, ds(tile[h * HALF + j] * w, w)]
                        v.tensor_tensor(m, m, bank[h][:, j * w:(j + 1) * w], ALU.max).then_inc(sweep_max, 1)

        def join_parts(v, st, s, w, dst):
            v.wait_ge(sweep_max, U + (s + 1) * VISITS)
            for k in range(3):
                st.link(v.tensor_tensor(dst[:, 0:TP * w], dst[:, 0:TP * w],
                                        ringf[:, 2560 + k * TP * HEADS:2560 + k * TP * HEADS + TP * w], ALU.max))

        EXPAND_AT, MINUS_AT = (2, 3, 4, 5), 6

        def expand(pe, i, h, r, b, w, nodes, regs, hh, visits=range(HALF), tile=None):
            if tile is None:
                tile = load_tiles(pe, regs, i, h * HALF, HALF)
                pe.wait_ge(ot_copied, i * 4 + (r * OT_PASS + 2 * h + 4))
                pe.wait_ge(weights_minus, i * 2 + (b * (2 * TURNS + 1) + h + 1))
            for j in visits:
                t = pe.matmul(bank[2 + hh][:, j * w:(j + 1) * w], onehotT[:, hh, j, :], nodes[:, ds(tile[j] * w, w)],
                              start=True, stop=True)
            if HALF - 1 in visits:
                t.then_inc(expand_ready, 1)
            return tile

        def weighted_tensor(pe, o, r, b, w, nodes, regs, main):
            turn_onehots(pe, 0, 0, o, r, 0)
            expand(pe, 0, 0, r, b, w, nodes, regs, 0)
            with pe.Fori(0, TURNS) as i:
                for h in range(2):
                    turn_onehots(pe, i, h + 1, o, r, 1 - h)
                    tile = None
                    for j in range(HALF):
                        if j in EXPAND_AT:
                            c = 2 * EXPAND_AT.index(j)
                            tile = expand(pe, i, h + 1, r, b, w, nodes, regs, 1 - h, (c, c + 1), tile)
                        main(pe, i, h, j)

        def attention_main(pe, i, h, j):
            k = h * HALF + j
            pe.wait_ge(rows_used, i * U + (U + VISITS + k + 1))
            pe.wait_ge(sums_added, i * U + (7 * VISITS + k + 1))
            s = bank[SBANK + j % SUM_BANKS]
            pe.matmul(s[:, 0:AW], onehot[:, k, :], ring[:, k, :], start=True, stop=True).then_inc(sums_ready, 1)

        def gat_main(pe, i, h, j):
            k = h * HALF + j
            pe.wait_ge(rows_in[k], i * 16 + 16 * (9 * TURNS + 1))
            pe.wait_ge(scaled_ready, i * U + (k + 1))
            pe.wait_ge(sums_added, i * U + (8 * VISITS + k + 1))
            s = bank[SBANK + j % SUM_BANKS]
            scaled = message[:, j % 4, 0:P]
            pe.matmul(s[:, 0:GW], scaled, ring[:, k, 0:GW], start=True, stop=True).then_inc(sums_ready, 1)

        def weighted_scalar(act, r, m, b):
            def exps(i, h, hh):
                act.wait_ge(weights_minus, i * 2 + (b * (2 * TURNS + 1) + h + 3))
                if b == 0:
                    to = ring[:, hh * HALF:(hh + 1) * HALF, D:AW]
                    x = minus[:, hh, :].rearrange("p (v h) -> p v h", h=HEADS)
                else:
                    to, x = weight[:, hh, :], minus[:, hh, 0:HALF]
                act.activation(to, x, ACT.Exp).then_inc(weights_ready, 1)
            copy_turned(act, 0, 0, r, m, 0)
            exps(0, 0, 0)
            with act.Fori(0, TURNS) as i:
                for h in range(2):
                    copy_turned(act, i, h + 1, r, m, 1 - h)
                    exps(i, h + 1, 1 - h)

        def attention_minus(v, st, i, h, hh):
            v.wait_ge(expand_ready, i * 2 + (h + 1))
            x = minus[:, hh, :]
            st.link(v.tensor_tensor(x, S[:, ds(i * (U * HEADS) + h * HALF * HEADS, HALF * HEADS)],
                                    bank[2 + hh][:, 0:HALF * HEADS], ALU.subtract))
            v.tensor_scalar(x, x, 0.0, None, ALU.min).then_inc(weights_minus, 1)

        def gat_minus(v, st, i, h, hh):
            v.wait_ge(expand_ready, i * 2 + (2 * TURNS + 1 + h + 1))
            x = minus[:, hh, 0:HALF]
            got = bank[2 + hh][:, 0:2 * HALF].rearrange("p (v k) -> p v k", k=2)
            st.link(v.tensor_tensor(x, asrc[:, ds(i * U + h * HALF, HALF)], got[:, :, 0], ALU.add))
            st.link(v.scalar_tensor_tensor(out=x, in0=x, scalar=0.2, in1=x, op0=ALU.mult, op1=ALU.max))
            st.link(v.tensor_tensor(x, x, got[:, :, 1], ALU.subtract))
            v.tensor_scalar(x, x, 0.0, None, ALU.min).then_inc(weights_minus, 1)

        def weighted_vector(v, st, b, m, aw, minus_, steps, prepare, regs):
            for j in range(U):
                build_onehot(v, 0, j, 0)
            minus_(v, st, 0, 0, 0)
            with v.Fori(0, TURNS) as i:
                st.enter(i, 2 * steps)
                tile = load_tiles(v, regs, i, 0, U)

                def add(k):
                    v.wait_ge(sums_ready, i * U + (U + m * VISITS + k + 1))
                    v.wait_ge(sums_added, i * U + (SUM_BANKS + (7 + b) * VISITS + k))
                    acc = ACC[:, ds(tile[k] * aw, aw)]
                    v.tensor_tensor(acc, acc, bank[SBANK + k % SUM_BANKS][:, 0:aw], ALU.add).then_inc(sums_added, 1)
                    build_onehot(v, i, k, U)

                for h in range(2):
                    v.wait_ge(weights_ready, i * 2 + (b * (2 * TURNS + 1) + h + 1))
                    for j in range(HALF):
                        prepare(v, i, h, j)
                        if j >= 2:
                            add(h * HALF + j - 2)
                        if j == MINUS_AT:
                            minus_(v, st, i, h + 1, 1 - h)
                    add(h * HALF + HALF - 2)
                    add(h * HALF + HALF - 1)
                st.leave(TURNS)

        def weigh_rows(v, i, h, j):
            k = h * HALF + j
            v.wait_ge(rows_in[k], i * 16 + 16 * (8 * TURNS + 1))
            rows = ring[:, k, 0:D].rearrange("p (h d) -> p h d", h=HEADS)
            v.tensor_tensor(rows, rows, ring[:, k, D:AW].unsqueeze(2).to_broadcast([P, HEADS, HD]),
                            ALU.mult).then_inc(rows_used, 1)

        def weigh_onehot(v, i, h, j):
            k = h * HALF + j
            v.tensor_scalar(message[:, j % 4, 0:P], onehot[:, k, :], weight[:, h, j:j + 1], None, ALU.mult
                            ).then_inc(scaled_ready, 1)

        SCALE = float(HD) ** -0.5
        kv_stage = S[:, 0:1024].rearrange("p (k u d) -> p k u d", k=2, u=2)

        def qkv_vector(v, q):
            with v.Fori(0, TP // 2) as i:
                for u in range(2):
                    v.wait_ge(d_product, i * 2 + (q * TP + u + 3))
                    v.wait_ge(kv_out[u], i * 32 + 32)
                    v.tensor_scalar(ACC[:, ds(i * (2 * D) + u * D, D)], bank[2 + u][:, 0:D], SCALE, None,
                                    ALU.mult)
                    v.tensor_copy(kv_stage[:, 0, u, :], bank[2 + u][:, D:2 * D])
                    v.tensor_copy(kv_stage[:, 1, u, :], bank[4 + u][:, 0:D]).then_inc(d_post, 1)

        def kv_sync(sp, q):
            for u in range(2):
                sp.sem_inc(kv_out[u], 32)
            with sp.Fori(0, TP // 2) as i:
                for u in range(2):
                    sp.wait_ge(d_post, i * 2 + (q * TP + u + 3))
                    for k, table in enumerate((k_table, v_table)):
                        sp.dma_start(table[ds(i * 2 * P + u * P, P), :], kv_stage[:, k, u, :]).then_inc(kv_out[u], 16)

        def y_of(t):
            return ACC[:, ds(t * D, D)]

        moments_f = moments[:, :, :].rearrange("p t s -> p (t s)")

        def attention_out(v, st, q):
            v.wait_ge(weights_ready, 2 * TURNS + 1)
            def heads_in(t, u):
                rec = small[:, 32 + 8 * u:40 + 8 * u]
                st.link(v.tensor_scalar(rec, ACC[:, ds(t * AW + D, HEADS)], 1e-8, None, ALU.add))
                st.link(v.reciprocal(rec, rec))
                v.tensor_tensor(pre[:, u, :].rearrange("p (h d) -> p h d", h=HEADS),
                                ACC[:, ds(t * AW, D)].rearrange("p (h d) -> p h d", h=HEADS),
                                rec.unsqueeze(2).to_broadcast([P, HEADS, HD]), ALU.mult).then_inc(d_pre, 1)

            def residual(t, u):
                st.link(v.tensor_tensor(mid[:, u, :], bank[2 + u][:, 0:D], bias["L2_gnn_Wo_b"][:, :], ALU.add))
                v.tensor_tensor(y_of(t), mid[:, u, :], x_of(t), ALU.add).then_inc(y_ready, 1)
                v.wait_ge(y_ready, t + 1)
                v.bn_stats(col(moments_f, t, 6), y_of(t)).then_inc(d_post, 1)

            after(v, st, q, 6, residual, heads_in)

        def norm_gain(v, st, i, src, gain):
            marks = [st.mark(v.tensor_scalar(mid[:, u, :], src(i * 2 + u), col(rstd, i * 2 + u), col(shift, i * 2 + u),
                                             ALU.mult, ALU.add)) for u in range(2)]
            for u in range(2):
                st.reached(marks[u])
                marks[u] = st.mark(v.tensor_tensor(mid[:, u, :], mid[:, u, :], gain, ALU.mult))
            return marks

        def norm_y(v, st, q):
            v.wait_ge(d_post, q * TP + 2)
            norm_factors(v, st)
            with v.Fori(0, TP // 2) as i:
                st.enter(i, 4)
                v.wait_ge(y_ready, i * 2 + TP)
                marks = norm_gain(v, st, i, y_of, bias["L2_gnn_ln1_g"][:, :])
                for u in range(2):
                    st.reached(marks[u])
                    v.tensor_tensor(y_of(i * 2 + u), mid[:, u, :], bias["L2_gnn_ln1_b"][:, :], ALU.add).then_inc(y_ready, 1)
                st.leave(TP // 2)

        def ffn_tensor(pe, q):
            def first(t, u):
                pe.wait_ge(d_evac, t + (q * TP + 3))
                pe.wait_ge(h_done, t + 1)
                for f in range(4):
                    for k in range(2):
                        m = pe.matmul(bank[2 + u][:, f * P:(f + 1) * P], fw1[:, k, f * P:(f + 1) * P],
                                      turned[:, u, k, :], start=(k == 0), stop=(k == 1))
                m.then_inc(h_product, 1)

            def second(t, u):
                pe.wait_ge(h_done, t + 3)
                pe.wait_ge(d_post, t + (q * TP + 1))
                for f in range(4):
                    m = pe.matmul(bank[4 + u][:, 0:D], hidden[:, u, f, :], fw2[:, f, :], start=(f == 0), stop=(f == 3))
                m.then_inc(d_product, 1)

            def body(t, last):
                for u in range(2):
                    if not last:
                        dense_turn(pe, q, D, t + (u + 2), u)
                    if not (last and u):
                        first(t + (u + 1), 1 - u)
                    second(t + u, u)

            pe.wait_ge(ffn_in, 32)
            pe.wait_ge(d_post, q * TP + 2)
            dense_turn(pe, q, D, 0, 0)
            dense_turn(pe, q, D, 1, 1)
            first(0, 0)
            by_pairs(pe, body)

        def ffn_scalar(act, q):
            def gelu(t, u):
                act.wait_ge(h_product, t + 1)
                act.wait_ge(d_product, t + (q * TP + 1))
                for f in range(4):
                    m = act.activation(hidden[:, u, f, :], bank[2 + u][:, f * P:(f + 1) * P], ACT.Gelu,
                                       bias=fb1[:, f:f + 1])
                m.then_inc(h_done, 1)

            def body(t, last):
                for u in range(2):
                    if not last:
                        act.wait_ge(h_product, t + (u + 1))
                        evacuate(act, q, D, ACT.Copy, t + (u + 2), u)
                    if not (last and u):
                        gelu(t + (u + 1), 1 - u)

            act.wait_ge(d_product, q * TP + 2)
            evacuate(act, q, D, ACT.Copy, 0, 0)
            evacuate(act, q, D, ACT.Copy, 1, 1)
            gelu(0, 0)
            by_pairs(act, body)

        def ffn_vector(v, st, q):
            v.wait_ge(y_ready, 2 * TP)
            with v.Fori(0, TP // 2) as i:
                st.enter(i, 4)
                for u in range(2):
                    t = i * 2 + u
                    v.wait_ge(d_product, i * 2 + (q * TP + u + 3))
                    st.link(v.tensor_tensor(mid[:, u, :], bank[4 + u][:, 0:D], bias["L2_gnn_ffn_b2"][:, :], ALU.add))
                    st.link(v.tensor_tensor(y_of(t), mid[:, u, :], y_of(t), ALU.add))
                    v.bn_stats(col(moments_f, t, 6), y_of(t)).then_inc(d_post, 1)
                st.leave(TP // 2)

        def block_residual(v, st, q):
            v.wait_ge(d_post, q * TP + 2)
            norm_factors(v, st)
            with v.Fori(0, TP // 2) as i:
                st.enter(i, 8)
                marks = norm_gain(v, st, i, y_of, bias["L2_gnn_ln2_g"][:, :])
                for u in range(2):
                    st.reached(marks[u])
                    marks[u] = st.mark(v.tensor_tensor(mid[:, u, :], mid[:, u, :], bias["L2_gnn_ln2_b"][:, :], ALU.add))
                for u in range(2):
                    st.reached(marks[u])
                    marks[u] = st.mark(v.tensor_tensor(x_of(i * 2 + u), mid[:, u, :], x_of(i * 2 + u), ALU.add))
                for u in range(2):
                    st.reached(marks[u])
                    v.bn_stats(col(moments_f, i * 2 + u, 6), x_of(i * 2 + u)).then_inc(y_ready, 1)
                st.leave(TP // 2)

        def xp_vector(v, q):
            with v.Fori(0, TP // 2) as i:
                for u in range(2):
                    t = i * 2 + u
                    v.wait_ge(d_product, i * 2 + (q * TP + u + 3))
                    v.tensor_copy(ACC[:, ds(t * GW, D)], bank[2 + u][:, 0:D])
                    v.tensor_copy(node_src[:, ds(t, 1)], bank[2 + u][:, D:D + 1])
                    v.tensor_copy(node_e[:, :, :].rearrange("p t k -> p (t k)")[:, ds(t * 2, 1)],
                                  bank[2 + u][:, D + 1:D + 2]).then_inc(d_post, 1)

        def xp_sync(sp, q):
            with sp.Fori(0, TP // 2) as i:
                sp.wait_ge(d_post, i * 2 + (q * TP + 4))
                sp.dma_start(xp_table[ds(i * 2 * P, 2 * P), :].rearrange("(t p) d -> p t d", p=P),
                             ACC[:, ds(i * 2 * GW, 2 * GW)].rearrange("p (t d) -> p t d", t=2)[:, :, 0:D]).then_inc(xp_out, 16)

        GQ = U // 4

        def sources_sync(sp):
            sp.sem_inc(tile_onehot_built, 2)
            with sp.Fori(0, TURNS // 2) as i:
                for b in range(2):
                    sp.wait_ge(tile_onehot_built, i * 2 + (b + 1))
                    sp.dma_start(src_hi[:, b, :], hi_rows[ds(i * 2 * U + b * U, U), :].rearrange("(o v) e -> o (v e)", o=1)
                                 .to_broadcast([TP, U * P])).then_inc(hi_in[b], 16)

        def sources_pool(pool):
            pool.sem_inc(row_looked_up, 2 * GQ)
            pool.wait_ge(src_rows_ready, 1)
            with pool.Fori(0, TURNS // 2) as i:
                for b in range(2):
                    pool.wait_ge(hi_in[b], i * 16 + 16)
                    pool.wait_ge(row_looked_up, i * (2 * GQ) + (b * GQ + GQ))
                    pool.sem_inc(tile_onehots_asked, 1)
                    pool.tensor_scalar(tile_onehot[:, b, :], src_hi[:, b, :], small[0:TP, 17:18], None, ALU.is_equal
                                       ).then_inc(tile_onehot_built, 1)

        def sources_tensor(pe):
            pe.sem_inc(src_taken, U)
            pe.wait_ge(src_rows_ready, 1)
            with pe.Fori(0, TURNS // 2) as i:
                for b in range(2):
                    pe.wait_ge(tile_onehot_built, i * 2 + (b + 3))
                    for q in range(GQ):
                        pe.wait_ge(src_taken, i * (2 * U) + (b * U + 4 * q + 4))
                        for c in range(4):
                            e = (4 * q + c) * P
                            t = pe.matmul(bank[SBANK + q][:, c * P:(c + 1) * P], tile_onehot[:, b, e:e + P],
                                          src_rows, start=True, stop=True)
                        t.then_inc(row_looked_up, 1)

        def sources_vector(v):
            with v.Fori(0, TURNS // 2) as i:
                for b in range(2):
                    for q in range(GQ):
                        v.wait_ge(row_looked_up, i * (2 * GQ) + (b * GQ + q + 1 + 2 * GQ))
                        v.wait_ge(src_taken, i * (2 * U) + (b * U + 4 * q + 4))
                        if q % 2 == 0:
                            v.wait_ge(src_copied, i * 4 + (2 * b + q // 2 + 1))
                        for c in range(4):
                            j = 4 * q + c
                            v.scalar_tensor_tensor(out=onehot[:, j, :], in0=iota[:, :],
                                                   scalar=src_lo[:, ds(i * (2 * U) + b * U + j, 1)],
                                                   in1=bank[SBANK + q][:, c * P:(c + 1) * P], op0=ALU.is_equal,
                                                   op1=ALU.mult, accum_out=src_now[:, j:j + 1]).then_inc(src_taken, 1)

        def sources_scalar(act):
            with act.Fori(0, TURNS) as i:
                for h in range(2):
                    act.wait_ge(src_taken, i * U + (U + HALF * (h + 1)))
                    act.copy(asrc[:, ds(i * U + h * HALF, HALF)], src_now[:, h * HALF:(h + 1) * HALF]).then_inc(src_copied, 1)

        def least_tensor(pe):
            pe.wait_ge(src_up, 1)
            pe.transpose(bank[0][0:TP, 0:P], node_src[:, :], ident[:, 0:P]).then_inc(src_turned, 1)
            pe.wait_ge(least_step, 1)
            pe.transpose(bank[2][0:1, 0:P], small[:, 50:51], ident[:, 0:P]).then_inc(least_turned, 1)
            pe.wait_ge(least_step, 2)
            pe.matmul(bank[3][:, 0:1], ones[0:1, :], small[0:1, 51:52], start=True, stop=True).then_inc(least_turned, 1)

        L3_GROUPS = [(0, 4), (4, VB - 4)]

        def gat_segment_tensor(pe):
            for g, (b0, nb) in enumerate(L3_GROUPS):
                pe.wait_ge(src_up, 2)
                if g:
                    pe.wait_ge(hs_out, GROUPS + g)
                for b in range(nb):
                    pe.transpose(bank[0][:, b * P:(b + 1) * P], asrc_up[:, (b0 + b) * P:(b0 + b + 1) * P], ident[:, 0:P])
                for b in range(nb):
                    t = pe.transpose(bank[1][:, b * P:(b + 1) * P], dloc[:, (b0 + b) * P:(b0 + b + 1) * P], ident[:, 0:P])
                t.then_inc(hs_turned, 1)
                pe.wait_ge(hs_done, GROUPS + g + 1)
                for b in range(nb):
                    t = pe.transpose(bank[2][:, b * P:(b + 1) * P], run[:, b * P:(b + 1) * P], ident[:, 0:P])
                t.then_inc(hs_back, 1)

        def gat_segment_scalar(act):
            for g, (b0, nb) in enumerate(L3_GROUPS):
                act.wait_ge(hs_turned, GROUPS + g + 2)
                act.copy(run[:, 0:nb * P], bank[0][:, 0:nb * P]).then_inc(hs_run, 1)
                act.wait_ge(hs_back, GROUPS + g + 1)
                act.copy(run_src[:, b0 * P:(b0 + nb) * P], bank[2][:, 0:nb * P]).then_inc(hs_out, 1)

        def gat_segment_vector(v, st):
            for g, (b0, nb) in enumerate(L3_GROUPS):
                v.wait_ge(hs_run, GROUPS + g + 1)
                st.link(v.tensor_copy(run_dst[:, 0:nb * P], bank[1][:, 0:nb * P]))
                running_max(v, st, blocks(run[:, 0:nb * P]), blocks(run_dst[:, 0:nb * P]), blocks(run_tmp[:, 0:nb * P]))
                v.tensor_copy(small[:, 30:31], run[:, 0:1]).then_inc(hs_done, 1)

        def gat_maxima_before(v, st, q):
            v.wait_ge(d_post, q * TP + 2)
            v.sem_inc(src_up, 1)
            v.wait_ge(src_turned, 1)
            v.tensor_copy(src_rows, bank[0][0:TP, 0:P]).then_inc(src_rows_ready, 1)
            v.tensor_reduce(small[:, 50:51], node_src[:, :], AX.X, ALU.min).then_inc(least_step, 1)
            v.wait_ge(least_turned, 1)
            v.tensor_reduce(small[0:1, 51:52], bank[2][0:1, 0:P], AX.X, ALU.min).then_inc(least_step, 1)
            v.wait_ge(least_turned, 2)
            st.link(v.tensor_copy(small[:, 52:53], bank[3][:, 0:1]))
            st.link(v.tensor_scalar(node_max[:, 0:TP], node_src[:, :], small[:, 52:53], None, ALU.subtract))
            st.link(v.memset(asrc[:, VISITS:VT], 0.0))
            st.link(v.tensor_scalar(asrc_up.bitcast(I32), idx_tab[:, :], P - 1, None, ALU.bitwise_and))
            st.link(v.tensor_copy(src_lo, asrc_up.bitcast(I32)))
            sources_vector(v)
            v.wait_ge(src_copied, 2 * TURNS + 2)
            v.tensor_scalar(asrc_up, asrc, small[:, 52:53], None, ALU.subtract).then_inc(src_up, 1)

        def gat_maxima_after(v, st):
            e_max, a_dst = node_e[:, :, 1], node_e[:, :, 0]
            st.link(v.tensor_scalar(node_max[:, 0:TP], node_max[:, 0:TP], small[:, 52:53], None, ALU.add))
            st.link(v.tensor_tensor(node_max[:, 0:TP], node_max[:, 0:TP], node_src[:, :], ALU.max))
            st.link(v.tensor_tensor(node_max[:, 0:TP], node_max[:, 0:TP], a_dst, ALU.add))
            st.link(v.scalar_tensor_tensor(out=e_max, in0=node_max[:, 0:TP], scalar=0.2, in1=node_max[:, 0:TP],
                                           op0=ALU.mult, op1=ALU.max))
            st.link(v.tensor_tensor(node_self, node_src[:, :], a_dst, ALU.add))
            st.link(v.scalar_tensor_tensor(out=node_self, in0=node_self, scalar=0.2, in1=node_self,
                                           op0=ALU.mult, op1=ALU.max))
            st.link(v.tensor_tensor(node_self, node_self, e_max, ALU.subtract))
            v.tensor_scalar(node_self, node_self, 0.0, None, ALU.min).then_inc(self_ready, 1)
            v.wait_ge(self_ready, 2)
            v.wait_ge(xp_out, 16 * (TP // 2))
            with v.Fori(0, TP) as t:
                v.tensor_scalar(ACC[:, ds(t * GW, D)], ACC[:, ds(t * GW, D)], node_self[:, ds(t, 1)], None, ALU.mult)
                v.tensor_copy(ACC[:, ds(t * GW + D, 1)], node_self[:, ds(t, 1)]).then_inc(acc_zero, 1)

        def gru_pairs(eng, body, st=None, per=0):
            with eng.Fori(0, TP // 2 - 2) as i:
                if st is not None:
                    st.enter(i, per)
                body(i * 2 + 1, 1)
                body(i * 2 + 2, 0)
                if st is not None:
                    st.leave(TP // 2 - 2)

        def gru_vector(v, st, q):
            def rows_in_(t, u):
                rec = small[:, 32 + u:33 + u]
                v.wait_ge(d_turned, t + (q * TP + 1))
                st.link(v.reciprocal(rec, ACC[:, ds(t * GW + D, 1)]))
                v.scalar_tensor_tensor(out=pre[:, u, :], in0=ACC[:, ds(t * GW, D)], scalar=rec,
                                       in1=bias["L3_gnn_bias"][:, :], op0=ALU.mult, op1=ALU.add).then_inc(d_pre, 1)

            def cell(t, u):
                v.wait_ge(gates_ready, t + 3)
                v.tensor_tensor(mid[:, u, :], gates[:, u, 0, :], gates[:, u, 1, :], ALU.mult).then_inc(cell_ready, 1)

            def output(t, u):
                v.wait_ge(cell_tanh, t + 1)
                st.link(v.tensor_tensor(mid[:, u, :], gates[:, u, 2, :], gates[:, u, 0, :], ALU.mult))
                st.link(v.tensor_tensor(x_of(t), mid[:, u, :], x_of(t), ALU.add))
                v.bn_stats(col(moments_f, t, 6), x_of(t)).then_inc(d_post, 1)

            def body(t, u):
                rows_in_(t + 2, u)
                cell(t, u)
                output(t + -1, 1 - u)

            rows_in_(0, 0)
            rows_in_(1, 1)
            rows_in_(2, 0)
            cell(0, 0)
            gru_pairs(v, body, st, 6)
            body(TP - 3, 1)
            cell(TP - 2, 0)
            output(TP - 3, 1)
            cell(TP - 1, 1)
            output(TP - 2, 0)
            output(TP - 1, 1)

        def gru_scalar(act, q):
            def turn(t, u):
                act.wait_ge(d_product, t + (q * TP + 1))
                evacuate(act, q, D, ACT.Tanh, t, u)

            def gate(t, u):
                act.wait_ge(d_product, t + (q * TP + 3))
                act.wait_ge(d_post, t + (q * TP + 1))
                act.activation(gates[:, u, 1, :], bank[2 + u][:, D:2 * D], ACT.Tanh)
                act.activation(gates[:, u, 0, :], bank[2 + u][:, 0:D], ACT.Sigmoid)
                act.activation(gates[:, u, 2, :], bank[4 + u][:, 0:D], ACT.Sigmoid).then_inc(gates_ready, 1)

            def cell(t, u):
                act.wait_ge(cell_ready, t + 1)
                act.activation(gates[:, u, 0, :], mid[:, u, :], ACT.Tanh).then_inc(cell_tanh, 1)

            def body(t, u):
                turn(t + 1, 1 - u)
                gate(t, u)
                cell(t + -1, 1 - u)

            turn(0, 0)
            turn(1, 1)
            gate(0, 0)
            gru_pairs(act, body)
            body(TP - 3, 1)
            body(TP - 2, 0)
            gate(TP - 1, 1)
            cell(TP - 2, 0)
            cell(TP - 1, 1)

        @block.sync
        def _(sp):
            setup_sync(sp)
            dbase = {0: (d_post, 2), 1: (d_post, TP + 2), 2: (d_post, 2 * TP + 2), 3: (h3_done, 0), 4: (d_post, 3 * TP + 2),
                     5: (d_post, 4 * TP + 2), 6: (t7_done, 0)}
            for p in range(7):
                done, base = dbase[p]
                table_sync(sp, done, base, tables[p], widths[p], accoff[p], table_out)
            for n, name in enumerate(("L2_gnn_Wq", "L2_gnn_Wk", "L2_gnn_Wv")):
                sp.dma_start(Wqkv[:, n], a[name].rearrange("(k p) n -> p k n", p=P)).then_inc(qkv_in, 16)
            kv_sync(sp, 7)
            sp.wait_ge(sums_added, SUM_BANKS + 8 * VISITS)
            sp.dma_start(fw1, a["L2_gnn_ffn_w1"].rearrange("(k p) n -> p k n", p=P)).then_inc(ffn_in, 16)
            sp.dma_start(fw2, a["L2_gnn_ffn_w2"].rearrange("(k p) n -> p k n", p=P)).then_inc(ffn_in, 16)
            xp_sync(sp, 10)
            sources_sync(sp)
            sp.wait_ge(x_ready, 4 * TP)
            sp.dma_start(out[0:(N // P) * P, :].rearrange("(t p) d -> p t d", p=P),
                         X[:, 0:(N // P) * D].rearrange("p (t d) -> p t d", d=D)).then_inc(out_done, 16)
            sp.dma_start(out[(N // P) * P:N, :], X[0:N % P, (TILES - 1) * D:TILES * D]).then_inc(out_done, 16)
            sp.wait_ge(out_done, 32)

        @block.gpsimd
        def _(pool):
            setup_pool(pool)
            pool.wait_ge(x_in, 32)
            bring(pool, 0, x_of, D)
            for p in range(7):
                gather_rows(pool, p, tables[p], widths[p], sums_ready, p * VISITS, 16 * (TP // 2) * (p + 1),
                            own_indices=False)
                if p >= 3:
                    pool.wait_ge(sums_added, SUM_BANKS + (p + 1) * VISITS)
                    bring(pool, p, acc_of(p), widths[p])

            bring(pool, 7, x_of, D, x_ready, TP)
            stored = 32 + 32 * (TP // 2)
            pool.wait_ge(kv_out[1], stored)
            gather_rows(pool, 7, k_table, D, rows_used, 0, stored, kv_out[0], own_indices=False)
            segment_pool(pool)
            pool.wait_ge(hs_out, GROUPS)
            pool.wait_ge(parts_joined, 1)
            gather_rows(pool, 8, v_table, D, sums_ready, 8 * VISITS, stored, kv_out[0])
            bring(pool, 9, y_of, D, y_ready, TP)
            bring(pool, 10, x_of, D, x_ready, 2 * TP)
            sources_pool(pool)
            pool.wait_ge(hs_out, GROUPS + len(L3_GROUPS))
            pool.wait_ge(parts_joined, 2)
            gather_rows(pool, 9, xp_table, D, sums_ready, 9 * VISITS, 16 * (TP // 2), xp_out)

        @block.tensor
        def _(pe):
            setup_tensor(pe)
            pe.wait_ge(weights_in, 16 * 8)
            pe.wait_ge(x_in, 32)
            pe.wait_ge(weight_copied, len(nat_blocks) + 1)
            dense_tensor(pe, 0, D, [lambda k: W1[:, k, :]], 128)
            sum_tensor(pe, 0, 0, 0, 0)
            dense_tensor(pe, 1, 128, [lambda k: W2[:, :]], 64)
            sum_tensor(pe, 1, 1, 1, OH_SUM)
            dense_tensor(pe, 2, 64, [lambda k: W3[:, :]], 32)
            sum_tensor(pe, 2, 2, 2, 2 * OH_SUM)
            sum_tensor(pe, 3, 3, 3, 3 * OH_SUM)
            dense_tensor(pe, 3, 32, [lambda k: W4[:, :]], 64)
            sum_tensor(pe, 4, 4, 4, 4 * OH_SUM)
            dense_tensor(pe, 4, 64, [lambda k: W5[:, :]], 128)
            sum_tensor(pe, 5, 5, 5, 5 * OH_SUM)
            dense_tensor(pe, 5, 128, [lambda k: W6[:, :]], 256)
            sum_tensor(pe, 6, 6, 6, 6 * OH_SUM)
            dense_tensor(pe, 6, 256, [lambda k: L1T[:, k, :]], 256)
            pe.wait_ge(qkv_in, 48)
            dense_tensor(pe, 7, 256, [lambda k, n=n: Wqkv[:, n, k, :] for n in range(3)], 256)
            regs = [pe.alloc_register(f"pe_tile{j}") for j in range(HALF)]
            o = 7 * OH_SUM
            score_tensor(pe, o, 0, 7, regs)
            o += OH_TWO
            segment_tensor(pe)
            pe.wait_ge(hs_out, GROUPS)
            sweep_tensor(pe, o, 0, HEADS, ACC)
            o += OH_SUM
            pe.wait_ge(acc_zero, 1)
            weighted_tensor(pe, o, 1, 0, HEADS, node_max, regs, attention_main)
            o += OH_TWO
            dense_tensor(pe, 8, 256, [lambda k: Wo[:, k, :]], 256)
            ffn_tensor(pe, 9)
            dense_tensor(pe, 10, 256, [lambda k: L3T[:, k, :]], 258)
            least_tensor(pe)
            sources_tensor(pe)
            gat_segment_tensor(pe)
            pe.wait_ge(hs_out, GROUPS + len(L3_GROUPS))
            sweep_tensor(pe, o, 1, 1, run_src)
            o += OH_SUM
            pe.wait_ge(acc_zero, 1 + TP)
            weighted_tensor(pe, o, 2, 1, 2, node_e[:, :, :].rearrange("p t k -> p (t k)"), regs, gat_main)
            dense_tensor(pe, 11, 256, [lambda k, n=n: WihT[:, k, n * D:(n + 1) * D] for n in range(3)], 256,
                         gates_ready)

        @block.scalar
        def _(act):
            setup_scalar(act)
            take_root(act, dis[:, 0:TILES], root[:, 0:TILES])
            dense_scalar(act, 0, D, ACT.Copy)
            indices_scalar(act, sums_ready, 0)
            dense_scalar(act, 1, 128, ACT.Relu)
            indices_scalar(act, sums_ready, VISITS)
            dense_scalar(act, 2, 64, ACT.Relu)
            indices_scalar(act, sums_ready, 2 * VISITS)
            indices_scalar(act, sums_ready, 3 * VISITS)
            dense_scalar(act, 3, 32, ACT.Copy)
            indices_scalar(act, sums_ready, 4 * VISITS)
            dense_scalar(act, 4, 64, ACT.Copy)
            indices_scalar(act, sums_ready, 5 * VISITS)
            dense_scalar(act, 5, 128, ACT.Copy)
            take_root(act, rstd[:, :], root[:, :])
            scale_rows(act, 6, t7_done)
            indices_scalar(act, sums_ready, 6 * VISITS)
            dense_scalar(act, 6, 256, ACT.Copy)
            take_root(act, rstd[:, :], root[:, :])
            dense_scalar(act, 7, 256, ACT.Copy)
            score_scalar(act, 0, 7)
            segment_scalar(act)
            weighted_scalar(act, 1, 8, 0)
            dense_scalar(act, 8, 256, ACT.Copy)
            take_root(act, rstd[:, :], root[:, :])
            ffn_scalar(act, 9)
            take_root(act, rstd[:, :], root[:, :])
            take_root(act, rstd[:, :], root[:, :])
            dense_scalar(act, 10, 256, ACT.Copy)
            sources_scalar(act)
            gat_segment_scalar(act)
            act.wait_ge(self_ready, 1)
            act.activation(node_self, node_self, ACT.Exp).then_inc(self_ready, 1)
            weighted_scalar(act, 2, 9, 1)
            gru_scalar(act, 11)
            take_root(act, rstd[:, :], root[:, :])

        @block.vector
        def _(v):
            st = Steps(v, vec)
            regs = [v.alloc_register(f"tile_reg{j}") for j in range(U)]
            setup_vector(v, st)
            v.wait_ge(bias_in, 16 * len(BIAS_W))
            after(v, st, 0, 0, product_scaled(v, 0))
            sum_vector(v, 0, 0, regs)
            after(v, st, 1, 0, product_scaled(v, 1), scaled_layer_in(v, 0, "L0_gnn_b1"))
            sum_vector(v, 1, 1, regs)
            after(v, st, 2, 0, product_scaled(v, 2), scaled_layer_in(v, 1, "L0_gnn_b2"))
            sum_vector(v, 2, 2, regs)
            twice_scaled(v, st, 2, "L0_gnn_b3", h3_done)
            sum_vector(v, 3, 3, regs)
            after(v, st, 3, 2, product_biased(v, st, 4, "L0_gnn_b4"))
            sum_vector(v, 4, 4, regs)
            after(v, st, 4, 2, product_biased(v, st, 5, "L0_gnn_b5"))
            sum_vector(v, 5, 5, regs)
            after(v, st, 5, 4, residual_in(v, st, "L0_gnn_b6", False))
            norm_x(v, st, 6)
            sum_vector(v, 6, 6, regs)
            after(v, st, 6, 6, residual_in(v, st, "L1_gnn_b", True))
            norm_x(v, st, 7)
            qkv_vector(v, 7)
            for u in range(2):
                v.wait_ge(kv_out[u], 32 + 32 * (TP // 2))
            v.memset(node_max[:, :], 0.0)
            score_vector(v, 7, 7)
            segment_vector(v, st)
            v.wait_ge(hs_out, GROUPS)
            sweep_vector(v, 0, HEADS, node_max, regs)
            join_parts(v, st, 0, HEADS, node_max)
            v.sem_inc(parts_joined, 1)
            v.memset(ACC[:, :], 0.0).then_inc(acc_zero, 1)
            weighted_vector(v, st, 0, 8, AW, attention_minus, 1, weigh_rows, regs)
            attention_out(v, st, 8)
            norm_y(v, st, 9)
            ffn_vector(v, st, 9)
            block_residual(v, st, 10)
            v.wait_ge(y_ready, 3 * TP)
            norm_x(v, st, 10)
            xp_vector(v, 10)
            gat_maxima_before(v, st, 11)
            gat_segment_vector(v, st)
            v.wait_ge(hs_out, GROUPS + len(L3_GROUPS))
            sweep_vector(v, 1, 1, node_max, regs)
            join_parts(v, st, 1, 1, node_max)
            v.memset(ring[:, :, D:GW], 1.0).then_inc(parts_joined, 1)
            gat_maxima_after(v, st)
            weighted_vector(v, st, 1, 9, GW, gat_minus, 3, weigh_onehot, regs)
            gru_vector(v, st, 11)
            norm_x(v, st, 12)


_INS = ['x', 'src', 'dst', 'L0_gnn_W1', 'L0_gnn_b1', 'L0_gnn_W2', 'L0_gnn_b2', 'L0_gnn_W3', 'L0_gnn_b3',
        'L0_gnn_W4', 'L0_gnn_b4', 'L0_gnn_W5', 'L0_gnn_b5', 'L0_gnn_W6', 'L0_gnn_b6', 'L1_gnn_W', 'L1_gnn_b',
        'L2_gnn_Wq', 'L2_gnn_Wk', 'L2_gnn_Wv', 'L2_gnn_Wo_w', 'L2_gnn_Wo_b', 'L2_gnn_ln1_g', 'L2_gnn_ln1_b',
        'L2_gnn_ln2_g', 'L2_gnn_ln2_b', 'L2_gnn_ffn_w1', 'L2_gnn_ffn_b1', 'L2_gnn_ffn_w2', 'L2_gnn_ffn_b2',
        'L3_gnn_W', 'L3_gnn_att_src', 'L3_gnn_att_dst', 'L3_gnn_bias', 'L3_gnn_W_ih', 'L3_gnn_W_hh']


def kernel(**inputs):
    import numpy as _np
    import concourse.bacc as _bacc
    from concourse import mybir as _mybir
    from concourse.bass_utils import run_bass_kernel_spmd as _run

    nc = _bacc.Bacc("TRN2", target_bir_lowering=False, num_devices=1)
    arrays, args = {}, {}
    for name in _INS:
        x = _np.ascontiguousarray(inputs[name])
        arrays[f"in_{name}_dram"] = x
        args[name] = nc.dram_tensor(f"in_{name}_dram", x.shape, _mybir.dt.from_np(x.dtype), kind="ExternalInput").ap()
    out = nc.dram_tensor("out_0_dram", (N, D), F32, kind="ExternalOutput").ap()
    build_program(nc, args, out)
    r = _run(nc, [arrays], core_ids=[0])
    return r.results[0]["out_0_dram"]
```
